# Optimizing a Trainium2 kernel written in Bass

```python
import numpy as np
import jax
import jax.numpy as jnp

def _softmax(x, axis=-1):
    return jax.nn.softmax(x, axis=axis)

def _gelu(x):
    return jax.nn.gelu(x, approximate=True)

def _silu(x):
    return jax.nn.silu(x)

def _sigmoid(x):
    return jax.nn.sigmoid(x)

def _layernorm(x, axis=-1, eps=1e-05):
    m = jnp.mean(x, axis=axis, keepdims=True)
    v = jnp.var(x, axis=axis, keepdims=True)
    return (x - m) / jnp.sqrt(v + eps)

def _scatter_add(tgt, idx, src, axis=0):
    return tgt.at[idx].add(src)

def _segment_sum(src, seg, n):
    return jax.ops.segment_sum(src, seg, n)
kernel_name = 'mk_xattn_ffn_d1_seqx_r4_8c8746'

def setup_inputs(seed: int=0):
    np.random.seed(seed)
    _w = jnp.asarray

    def _rec_inputs():
        import jax
        import jax.numpy as jnp
        _rk = jax.random.key(seed)
        x = -0.0005207 + 1.001 * jax.random.normal(jax.random.fold_in(_rk, 1), (16, 256, 256), jnp.float32)
        _lenS = 256 - jax.random.randint(jax.random.fold_in(_rk, 7), (16,), 0, max(1, 256 // 4) + 1, jnp.int32)
        _lenS2 = 120 - jax.random.randint(jax.random.fold_in(_rk, 8), (16,), 0, max(1, 120 // 4) + 1, jnp.int32)
        _ctx_1024P = jax.random.normal(jax.random.fold_in(_rk, 11), (16, 16, 256), jnp.float32)
        _ctx_1024c = jax.random.dirichlet(jax.random.fold_in(_rk, 511), 0.3 * jnp.ones((16,), jnp.float32), (16, 120))
        _ctx_1024t = jnp.einsum('bsk,bkd->bsd', _ctx_1024c, _ctx_1024P)
        _ctx_1024t = _ctx_1024t * jax.lax.rsqrt(jnp.mean(jnp.square(_ctx_1024t)) + 1e-12) * 0.953939
        ctx_1024 = -1.39393e-06 + 0.999914 * (_ctx_1024t + 0.3 * jax.random.normal(jax.random.fold_in(_rk, 611), (16, 120, 256), jnp.float32))
        return (x, ctx_1024)
    x, ctx_1024 = _rec_inputs()

    def _L0_xattn_setup():
        import jax, jax.numpy as jnp
        import numpy as np
        EMBED_DIM = 256
        NUM_HEADS = 16
        HEAD_DIM = EMBED_DIM // NUM_HEADS
        SCALE = HEAD_DIM ** (-0.5)
        key = jax.random.key(seed)
        ks = jax.random.split(key, 8)
        B, Nq, Nkv, C = (2, 256, 512, EMBED_DIM)
        xavier = (6.0 / (C + C)) ** 0.5

        def w(k):
            return jax.random.uniform(k, (C, C), jnp.float32, -xavier, xavier)
        return {'query': jax.random.normal(ks[0], (B, Nq, C), jnp.float32), 'key': jax.random.normal(ks[1], (B, Nkv, C), jnp.float32), 'value': jax.random.normal(ks[2], (B, Nkv, C), jnp.float32), 'Wq': w(ks[3]), 'bq': jnp.zeros((C,), jnp.float32), 'Wk': w(ks[4]), 'bk': jnp.zeros((C,), jnp.float32), 'Wv': w(ks[5]), 'bv': jnp.zeros((C,), jnp.float32), 'Wo': w(ks[6]), 'bo': jnp.zeros((C,), jnp.float32), 'temperature': jnp.ones((NUM_HEADS, 1, 1), jnp.float32)}
    _L0_xattn_all = _L0_xattn_setup()
    _L0_xattn_in = {k: v for k, v in _L0_xattn_all.items() if k in ('Wq', 'bq', 'Wk', 'bk', 'Wv', 'bv', 'Wo', 'bo', 'temperature')}
    del _L0_xattn_all

    def _L0_ffn_setup():
        import jax, jax.numpy as jnp
        import numpy as np
        DIM = 256
        HIDDEN = 768
        SCALE = 1.0 / 127.0

        def _dequant(w_int, dtype):
            return w_int.astype(dtype) * jnp.asarray(SCALE, dtype)
        key = jax.random.key(seed)
        k_x, k_g, k_u, k_d = jax.random.split(key, 4)
        x = jax.random.normal(k_x, (4, 512, DIM), dtype=jnp.float32)
        w_gate = jax.random.randint(k_g, (HIDDEN, DIM), -127, 128, dtype=jnp.int32)
        w_up = jax.random.randint(k_u, (HIDDEN, DIM), -127, 128, dtype=jnp.int32)
        w_down = jax.random.randint(k_d, (DIM, HIDDEN), -127, 128, dtype=jnp.int32)
        return {'x': x, 'w_gate': w_gate, 'w_up': w_up, 'w_down': w_down}
    _L0_ffn_all = _L0_ffn_setup()
    _L0_ffn_in = {k: v for k, v in _L0_ffn_all.items() if k in ('w_gate', 'w_up', 'w_down')}
    del _L0_ffn_all
    return {'x': x, 'ctx_1024': ctx_1024, 'L0_xattn_Wq': _L0_xattn_in['Wq'], 'L0_xattn_bq': _L0_xattn_in['bq'], 'L0_xattn_Wk': _L0_xattn_in['Wk'], 'L0_xattn_bk': _L0_xattn_in['bk'], 'L0_xattn_Wv': _L0_xattn_in['Wv'], 'L0_xattn_bv': _L0_xattn_in['bv'], 'L0_xattn_Wo': _L0_xattn_in['Wo'], 'L0_xattn_bo': _L0_xattn_in['bo'], 'L0_xattn_temperature': _L0_xattn_in['temperature'], 'L0_ffn_w_gate': _L0_ffn_in['w_gate'], 'L0_ffn_w_up': _L0_ffn_in['w_up'], 'L0_ffn_w_down': _L0_ffn_in['w_down']}

def reference(x, ctx_1024, L0_xattn_Wq, L0_xattn_bq, L0_xattn_Wk, L0_xattn_bk, L0_xattn_Wv, L0_xattn_bv, L0_xattn_Wo, L0_xattn_bo, L0_xattn_temperature, L0_ffn_w_gate, L0_ffn_w_up, L0_ffn_w_down):
    import jax
    import jax.numpy as jnp

    def _L0_xattn_ref(query, key, value, Wq, bq, Wk, bk, Wv, bv, Wo, bo, temperature):
        import jax, jax.numpy as jnp
        import numpy as np
        EMBED_DIM = 256
        NUM_HEADS = 16
        HEAD_DIM = EMBED_DIM // NUM_HEADS
        SCALE = HEAD_DIM ** (-0.5)
        B, Nq, C = query.shape
        Nkv = key.shape[1]
        H, D = (NUM_HEADS, HEAD_DIM)
        Q = (query @ Wq.T + bq).reshape(B, Nq, H, D).transpose(0, 2, 1, 3)
        K = (key @ Wk.T + bk).reshape(B, Nkv, H, D).transpose(0, 2, 1, 3)
        V = (value @ Wv.T + bv).reshape(B, Nkv, H, D).transpose(0, 2, 1, 3)
        scores = jnp.einsum('bhqd,bhkd->bhqk', Q, K) * SCALE
        scores = scores / temperature
        attn = jax.nn.softmax(scores, axis=-1)
        out = jnp.einsum('bhqk,bhkd->bhqd', attn, V)
        out = out.transpose(0, 2, 1, 3).reshape(B, Nq, C)
        return out @ Wo.T + bo

    def _L0_ffn_ref(x, w_gate, w_up, w_down):
        import jax, jax.numpy as jnp
        import numpy as np
        DIM = 256
        HIDDEN = 768
        SCALE = 1.0 / 127.0

        def _dequant(w_int, dtype):
            return w_int.astype(dtype) * jnp.asarray(SCALE, dtype)
        wg = _dequant(w_gate, x.dtype)
        wu = _dequant(w_up, x.dtype)
        wd = _dequant(w_down, x.dtype)
        gate = jnp.einsum('bsd,hd->bsh', x, wg)
        up = jnp.einsum('bsd,hd->bsh', x, wu)
        h = jax.nn.silu(gate) * up
        return jnp.einsum('bsh,dh->bsd', h, wd)
    x = x + _L0_xattn_ref(_layernorm(x, axis=-1), ctx_1024, ctx_1024, L0_xattn_Wq, L0_xattn_bq, L0_xattn_Wk, L0_xattn_bk, L0_xattn_Wv, L0_xattn_bv, L0_xattn_Wo, L0_xattn_bo, L0_xattn_temperature)
    x = x + _L0_ffn_ref(_layernorm(x, axis=-1), L0_ffn_w_gate, L0_ffn_w_up, L0_ffn_w_down)
    return x

_drawn_inputs = setup_inputs


def setup_inputs(seed=0):
    import zlib

    import numpy as np

    out = dict(_drawn_inputs(seed))
    spreads = {'L0_xattn_bq': (0.0, 0.1),
     'L0_xattn_bk': (0.0, 0.1),
     'L0_xattn_bv': (0.0, 0.1),
     'L0_xattn_bo': (0.0, 0.1),
     'L0_xattn_temperature': (1.0, 0.2)}
    factors = {}
    for name, (base, spread) in spreads.items():
        noise = np.random.default_rng([zlib.crc32(name.encode()), seed]).standard_normal(out[name].shape)
        drawn = base * np.exp(spread * noise) if base else spread * noise
        out[name] = jnp.asarray(drawn.astype(out[name].dtype))
    for name, factor in factors.items():
        out[name] = (out[name] * factor).astype(out[name].dtype)
    return out
```

```python
import concourse.bass as bass
from concourse import mybir
from contextlib import ExitStack

F32 = mybir.dt.float32
F32R = mybir.dt.float32r
I32 = mybir.dt.int32
ALU = mybir.AluOpType
ACT = mybir.ActivationFunctionType
AX = mybir.AxisListType

P = 128
RING = 3
FIRST, LAST = -3, 18
LOOP_FROM, LOOP_TURNS = 4, 3

JOBS = [
    (0, "shift", 0, 0),
    (1, "normT2", 0, -2), (1, "down", 0, -3),
    (2, "down", 1, -3), (2, "gateup", 0, -2),
    (3, "normT1", 0, 2), (3, "gateup", 1, -2),
    (4, "gateup", 2, -2), (4, "q", 0, 2),
    (5, "attT", 0, -1), (5, "gateup", 3, -2),
    (6, "k", 0, 2), (6, "gateup", 4, -2),
    (7, "v", 0, 2), (7, "wo", 0, -1), (7, "gateup", 5, -2),
]
STEPS = 8


class Batch:

    def __init__(self, loop, c):
        self.loop, self.c = loop, c

    def __add__(self, d):
        return Batch(self.loop, self.c + d)

    @property
    def slot(self):
        return self.c % RING

    def exists(self, n_batches):
        return self.loop is not None or 0 <= self.c < n_batches

    def count(self, per, k):
        c = self.c * per + k
        assert self.loop is None or c > 0, (self.c, per, k)
        return c if self.loop is None else self.loop * (RING * per) + c

    def slot_count(self, per, k):
        c = (self.c // RING) * per + k
        assert self.loop is None or c > 0, (self.c, per, k)
        return c if self.loop is None else self.loop * per + c

    def number(self):
        return self.c if self.loop is None else self.loop * RING + self.c


def at_least(eng, sem, value):
    if not (isinstance(value, int) and value <= 0):
        eng.wait_ge(sem, value)


def turns(eng, turn):
    for c in range(FIRST, LOOP_FROM):
        turn(Batch(None, c))
    with eng.Fori(0, LOOP_TURNS) as j:
        for u in range(RING):
            turn(Batch(j, LOOP_FROM + u))
    for c in range(LOOP_FROM + RING * LOOP_TURNS, LAST + 1):
        turn(Batch(None, c))


def build(nc, x, ctx, wqT, bq, wkT, bk, wvT, bv, woT, bo, temp, tempc, wgT, wuT, wdT, out):
    NB, NQ, C = x.shape
    NKV = ctx.shape[2]
    H = temp.shape[0]
    D = C // H
    HID = wgT.shape[1]
    CC = C // P
    QT = NQ // P
    HC = H // CC
    FC = HID // P
    VW = D + 1
    SCALE = float(D) ** -0.5
    EPS = 1e-5
    DEQ = 1.0 / 127.0
    HG = 2
    AG = H * QT // STEPS
    WEIGHT_LOADS = 4 + 6
    KS_ROWS = 3 * D
    assert CC == 2 and QT == 2 and H * 16 == C and FC == 6 and NB == 16
    assert H == HG * STEPS and AG * NKV <= 512

    es = ExitStack()
    with es:
        def sb(name, shape, dt=F32):
            return es.enter_context(nc.sbuf_tensor(name, shape, dt))

        def psum(name, shape):
            return es.enter_context(nc.psum_tensor(name, shape, F32))

        def sem(name):
            return es.enter_context(nc.semaphore(name))

        wq = sb("wq", [P, 2, CC, C], F32R)
        wk = sb("wk", [P, 2, CC, C], F32R)
        wv = sb("wv", [P, 2, CC, C], F32R)
        wo = sb("wo", [P, 2, CC, C], F32R)
        wg = sb("wg", [P, 2, CC, HID], F32R)
        wu = sb("wu", [P, 2, CC, HID], F32R)
        wd = sb("wd", [P, 2, FC, C], F32R)
        temp_row = sb("temp_row", [P, H])
        temp_col = sb("temp_col", [P, CC])
        bq_col = sb("bq_col", [P, CC])
        bk_col = sb("bk_col", [P, CC])
        bv_row = sb("bv_row", [P, C])
        bo_row = sb("bo_row", [P, C])
        ident = sb("ident", [P, P])
        minus_half = sb("minus_half", [P, QT])
        eps_col = sb("eps_col", [P, QT])

        x_tok = sb("x_tok", [P, RING, QT, C])
        x_res = sb("x_res", [P, RING, QT, C])
        ctx_raw = sb("ctx_raw", [P, RING, CC, NKV])
        ctxT = sb("ctxT", [P, 2, CC, NKV], F32R)
        stats = sb("stats", [P, 2, QT, 6])
        meanvar = sb("meanvar", [P, 2, QT, 2])
        vareps = sb("vareps", [P, 2, QT])
        rstd = sb("rstd", [P, 2, QT])
        xn1 = sb("xn1", [P, QT, C])
        xn2 = sb("xn2", [P, QT, C])
        xn1T = sb("xn1T", [P, 2, CC, NQ], F32R)
        xn2T = sb("xn2T", [P, 2, CC, NQ], F32R)
        qT = sb("qT", [P, 2, CC, NQ], F32R)
        kT = sb("kT", [P, 2, CC, NKV], F32R)
        qs = [sb(f"qs{r}", [KS_ROWS + 2, H, NQ], F32R) for r in range(RING)]
        ks = [sb(f"ks{r}", [KS_ROWS + 2, H, NKV], F32R) for r in range(RING)]
        v_one = [sb(f"v_one{r}", [NKV, H, VW]) for r in range(RING)]
        negmax = sb("negmax", [P, RING, QT, H])
        shiftT = sb("shiftT", [H, 2, NQ], F32R)
        probs = sb("probs", [P, 4, HG * NQ])
        rsum = sb("rsum", [P, QT, H])
        att = sb("att", [P, QT, C])
        attT = sb("attT", [P, 2, CC, NQ], F32R)
        x1 = sb("x1", [P, RING, QT, C])
        tanh_g = sb("tanh_g", [P, 2, NQ])
        hid = sb("hid", [P, 2, NQ])
        hidT = sb("hidT", [P, 2, FC, NQ], F32R)
        y = sb("y", [P, RING, QT, C])
        raw_w = probs[:].rearrange("p a (b c) -> p a b c", c=C)
        raw_i = y[:].bitcast(I32).rearrange("p r t c -> p (r t c)")
        raw_f = x1[:].rearrange("p r t c -> p (r t c)")

        ps_a = [psum(f"ps_a{b}", [P, 512]) for b in range(2)]
        ps_b = [psum(f"ps_b{b}", [P, 512]) for b in range(2)]
        ps_o = psum("ps_o", [P, QT, 512])
        ps_w = [psum(f"ps_w{b}", [P, 512]) for b in range(2)]

        weights_in = sem("weights_in")
        gate_in, up_in, down_in = sem("gate_in"), sem("up_in"), sem("down_in")
        x_in = [sem(f"x_in{r}") for r in range(RING)]
        xres_in = [sem(f"xres_in{r}") for r in range(RING)]
        ctx_in = [sem(f"ctx_in{r}") for r in range(RING)]
        qs_in = [sem(f"qs_in{r}") for r in range(RING)]
        ks_in = [sem(f"ks_in{r}") for r in range(RING)]
        shift_in = [sem(f"shift_in{r}") for r in range(RING)]
        stored = [sem(f"stored{r}") for r in range(RING)]
        consts_done = sem("consts_done")
        ident_done = sem("ident_done")
        prep_done = sem("prep_done")
        gint_f, gint_hi, gint_lo = sem("gint_f"), sem("gint_hi"), sem("gint_lo")
        full = {k: sem(f"{k}_full") for k in ("shift", "normT2", "down", "gateup", "normT1", "q", "attT", "k", "v", "wo")}
        a_full, b_full, pv_done = sem("a_full"), sem("b_full"), sem("pv_done")
        hi = {k: sem(f"{k}_hi") for k in ("shift", "normT2", "normT1", "q", "attT", "k", "ctx", "hid")}
        exp_done, tanh_done = sem("exp_done"), sem("tanh_done")
        emptied = {k: sem(f"{k}_emptied") for k in ("shift", "normT2", "down", "gateup", "normT1", "q", "attT", "k", "v", "wo")}
        a_max, rsum_done, att_done = sem("a_max"), sem("rsum_done"), sem("att_done")
        stats1, stats2 = sem("stats1"), sem("stats2")
        var1, var2 = sem("var1"), sem("var2")
        xn1_done, xn2_done = sem("xn1_done"), sem("xn2_done")
        gated_done = sem("gated_done")
        eps1, eps2 = sem("eps1"), sem("eps2")
        rstd1, rstd2 = sem("rstd1"), sem("rstd2")
        ctx_lo, hid_lo, xres_done = sem("ctx_lo"), sem("hid_lo"), sem("xres_done")

        per_batch = {"gateup": FC, "down": QT}

        def job_count(kind, idx, n):
            return n.count(per_batch.get(kind, 1), idx + 1)

        def job_before(pos, i):
            back = 0
            while True:
                pos -= 2
                if pos < 0:
                    pos, back = pos + len(JOBS), back + 1
                if (i + -back).c < FIRST - 1:
                    return None
                _, kind, idx, off = JOBS[pos]
                n = i + (off - back)
                if n.exists(NB):
                    return kind, idx, n

        def bank_of(kind, idx):
            return next(ps_w[pos % 2] for pos, (_, k, x_, _) in enumerate(JOBS) if (k, x_) == (kind, idx))

        def second_pass(i, g):
            return (i, g - 4) if g >= 4 else (i + -1, g + 4)

        block = es.enter_context(nc.Block())

        @block.sync
        def _(sp):
            def row(v):
                return v.rearrange("(a n) -> a n", a=1)

            for k, w in enumerate((wqT, wkT, wvT, woT)):
                sp.dma_start(raw_w[:, k], w.rearrange("(c p) n -> p c n", p=P)).then_inc(weights_in, 16)
            small = [
                (temp_row[:], temp.rearrange("h a b -> (a b) h").to_broadcast([P, H])),
                (bv_row[:], row(bv).to_broadcast([P, C])),
                (bo_row[:], row(bo).to_broadcast([P, C])),
                (bq_col[:], bq),
                (bk_col[:], bk),
                (temp_col[:], tempc),
            ]
            for dst, src in small:
                sp.dma_start(dst, src).then_inc(weights_in, 16)
            def turn(i):
                n = i + 3
                if n.exists(NB):
                    at_least(sp, xn1_done, (n + -RING).count(1, 1))
                    sp.dma_start(x_tok[:, n.slot], x[n.number()].rearrange("(t p) c -> p t c", p=P)).then_inc(x_in[n.slot], 16)
                    at_least(sp, ctx_lo, (n + -RING).count(1, 1))
                    sp.dma_start(ctx_raw[:, n.slot], ctx[n.number()].rearrange("(c p) k -> p c k", p=P)).then_inc(ctx_in[n.slot], 16)
                n = i
                if n.exists(NB):
                    at_least(sp, emptied["wo"], (n + -RING).count(1, 1))
                    sp.dma_start(x_res[:, n.slot], x[n.number()].rearrange("(t p) c -> p t c", p=P)).then_inc(xres_in[n.slot], 16)
                    sp.wait_ge(emptied["shift"], n.count(1, 1))
                    for part in range(2):
                        sp.dma_start(qs[n.slot].bitcast(F32)[KS_ROWS + part:KS_ROWS + part + 1], shiftT.bitcast(F32)[:, part]).then_inc(shift_in[n.slot], 16)
                n = i + -3
                if n.exists(NB):
                    sp.wait_ge(emptied["down"], n.count(QT, QT))
                    sp.dma_start(out[n.number()].rearrange("(t p) c -> p t c", p=P), y[:, n.slot]).then_inc(stored[n.slot], 16)
                n = i + 2
                if n.exists(NB):
                    for kind, t, stack, arrived, parts in (("q", qT, qs, qs_in, (0, 1, 0)), ("k", kT, ks, ks_in, (0, 0, 1))):
                        at_least(sp, b_full, (n + -RING).count(STEPS, STEPS))
                        sp.wait_ge(emptied[kind], n.count(1, 1))
                        for r, part in enumerate(parts):
                            for c in range(CC):
                                sp.dma_start(
                                    stack[n.slot].bitcast(F32)[r * D:(r + 1) * D, c * HC:(c + 1) * HC, :],
                                    t.bitcast(F32)[:, part, c, :]).then_inc(arrived[n.slot], 16)

            for r in range(RING):
                sp.sem_inc(stored[r], 16)
            turns(sp, turn)
            for r in range(RING):
                sp.wait_ge(stored[r], 16 * (1 + len(range(r, NB, RING))))

        @block.gpsimd
        def _(pool):
            nc.gpsimd.memset(ident[:], 0.0).then_inc(ident_done, 1)
            pool.wait_ge(ident_done, 1)
            nc.gpsimd.affine_select(out=ident[:], in_=ident[:], compare_op=ALU.not_equal, fill=1.0, base=0,
                                    pattern=[[-1, P]], channel_multiplier=1).then_inc(ident_done, 1)
            nc.gpsimd.memset(minus_half[:], -0.5)
            nc.gpsimd.memset(eps_col[:], EPS)
            for r in range(RING):
                nc.gpsimd.memset(v_one[r][:], 1.0)
                last = nc.gpsimd.memset(ks[r].bitcast(F32)[:], 1.0)
            last.then_inc(consts_done, 1)
            pool.wait_ge(consts_done, 1)

            def integer_weight_lo(k, w):
                pool.wait_ge(gint_hi, k + 1)
                flat = w[:, 1].rearrange("p c n -> p (c n)")
                nc.gpsimd.tensor_tensor(flat, raw_f, w[:, 0].bitcast(F32).rearrange("p c n -> p (c n)"),
                                        ALU.subtract).then_inc(gint_lo, 1)

            def rsqrt(which, n, got, eps_sem, out_sem):
                pool.wait_ge(got, n.count(1, 1))
                nc.gpsimd.tensor_tensor(vareps[:, which], meanvar[:, which, :, 1], eps_col[:], ALU.add).then_inc(eps_sem, 1)
                pool.wait_ge(eps_sem, n.count(1, 1))
                nc.gpsimd.tensor_tensor(rstd[:, which], vareps[:, which], minus_half[:], ALU.pow).then_inc(out_sem, 1)

            def hidden_lo(n, f):
                pool.wait_ge(hi["hid"], n.count(FC, f + 1))
                nc.gpsimd.tensor_tensor(hidT[:, 1, f], hid[:, f % 2], hidT[:, 0, f].bitcast(F32), ALU.subtract).then_inc(hid_lo, 1)

            def turn(i):
                if i.loop is None and FIRST <= i.c < FIRST + 3:
                    integer_weight_lo(i.c - FIRST, (wg, wu, wd)[i.c - FIRST])
                if (i + -3).exists(NB):
                    hidden_lo(i + -3, FC - 1)
                n = i + 2
                if n.exists(NB):
                    rsqrt(0, n, var1, eps1, rstd1)
                    pool.wait_ge(hi["ctx"], n.count(1, 1))
                    nc.gpsimd.tensor_tensor(ctxT[:, 1], ctx_raw[:, n.slot], ctxT[:, 0].bitcast(F32), ALU.subtract).then_inc(ctx_lo, 1)
                n = i
                if n.exists(NB):
                    pool.wait_ge(xres_in[n.slot], n.slot_count(1, 1) * 16)
                    if n.c == 0:
                        pool.wait_ge(weights_in, 16 * WEIGHT_LOADS)
                    for t in range(QT):
                        last = nc.gpsimd.tensor_tensor(x_res[:, n.slot, t], x_res[:, n.slot, t], bo_row[:], ALU.add)
                    last.then_inc(xres_done, 1)
                if (i + -2).exists(NB):
                    for f in range(FC - 1):
                        hidden_lo(i + -2, f)
                if (i + -1).exists(NB):
                    rsqrt(1, i + -1, var2, eps2, rstd2)

            turns(pool, turn)

        @block.scalar
        def _(act):
            act.dma_start(raw_i.rearrange("p (c n) -> p c n", c=CC), wgT.rearrange("(c p) n -> p c n", p=P)).then_inc(gate_in, 16)

            def integer_weight(k):
                arrived, w = ((gate_in, wg), (up_in, wu), (down_in, wd))[k]
                act.wait_ge(arrived, 16)
                at_least(act, gint_lo, k)
                nc.scalar.activation(raw_f, raw_i, ACT.Copy).then_inc(gint_f, 1)
                act.wait_ge(gint_f, k + 1)
                nc.scalar.activation(w[:, 0].rearrange("p c n -> p (c n)"), raw_f, ACT.Copy).then_inc(gint_hi, 1)
                if k == 0:
                    act.dma_start(raw_i.rearrange("p (c n) -> p c n", c=CC), wuT.rearrange("(c p) n -> p c n", p=P)).then_inc(up_in, 16)
                if k == 1:
                    act.dma_start(raw_i.rearrange("p (c n) -> p c n", c=FC), wdT.rearrange("(c p) n -> p c n", p=P)).then_inc(down_in, 16)

            def high(kind, n, dst, src):
                act.wait_ge(full[kind], n.count(1, 1))
                nc.scalar.activation(dst, src, ACT.Copy).then_inc(hi[kind], 1)

            def hidden_hi(n, f):
                if f == 0:
                    at_least(act, full["down"], (n + -1).count(QT, QT))
                act.wait_ge(emptied["gateup"], n.count(FC, f + 1))
                nc.scalar.activation(hidT[:, 0, f], hid[:, f % 2], ACT.Copy).then_inc(hi["hid"], 1)

            def turn(i):
                if i.loop is None and FIRST <= i.c < FIRST + 3:
                    integer_weight(i.c - FIRST)
                for g in range(STEPS):
                    n, gb = second_pass(i, g)
                    if n.exists(NB):
                        at_least(act, pv_done, n.count(STEPS, gb + 1 - 4))
                        act.wait_ge(b_full, n.count(STEPS, gb + 1))
                        nc.scalar.activation(probs[0:NKV, gb % 4], ps_b[gb % 2][0:NKV], ACT.Exp).then_inc(exp_done, 1)
                    if g == 0:
                        if (i + -3).exists(NB):
                            hidden_hi(i + -3, FC - 1)
                        if i.exists(NB):
                            if not (i.loop is None and i.c == 0):
                                act.wait_ge(shift_in[(i + -1).slot], (i + -1).slot_count(1, 1) * 32)
                            act.wait_ge(full["shift"], i.count(1, 1))
                            nc.scalar.activation(shiftT[:, 0], bank_of("shift", 0)[0:H, 0:NQ], ACT.Copy).then_inc(hi["shift"], 1)
                    if g == 1:
                        n = i + -2
                        if n.exists(NB):
                            at_least(act, full["gateup"], (n + -1).count(FC, FC))
                            high("normT2", n, xn2T[:, 0].rearrange("p c q -> p (c q)"), bank_of("normT2", 0)[:])
                        n = i + 2
                        if n.exists(NB):
                            act.wait_ge(ctx_in[n.slot], n.slot_count(1, 1) * 16)
                            at_least(act, full["v"], (n + -1).count(1, 1))
                            nc.scalar.activation(ctxT[:, 0], ctx_raw[:, n.slot], ACT.Copy).then_inc(hi["ctx"], 1)
                    if g == 3 and (i + 2).exists(NB):
                        at_least(act, full["q"], (i + 1).count(1, 1))
                        high("normT1", i + 2, xn1T[:, 0].rearrange("p c q -> p (c q)"), bank_of("normT1", 0)[:])
                    if g == 5 and (i + -1).exists(NB):
                        at_least(act, full["wo"], (i + -2).count(1, 1))
                        high("attT", i + -1, attT[:, 0].rearrange("p c q -> p (c q)"), bank_of("attT", 0)[:])
                    n = i + -2
                    if g >= 2 and n.exists(NB):
                        f = g - 2
                        act.wait_ge(full["gateup"], n.count(FC, f + 1))
                        at_least(act, gated_done, n.count(FC, f - 1))
                        nc.scalar.activation(tanh_g[:, f % 2], bank_of("gateup", f)[:, 0:NQ], ACT.Tanh, scale=DEQ / 2).then_inc(tanh_done, 1)
                        if f >= 1:
                            hidden_hi(n, f - 1)
                    if (g == 4 or g == 6) and (i + 2).exists(NB):
                        n = i + 2
                        kind, t, w, bias, arrived = ("q", qT, NQ, bq_col, qs_in) if g == 4 else ("k", kT, NKV, bk_col, ks_in)
                        if not (n.loop is None and n.c == 0):
                            act.wait_ge(arrived[(n + -1).slot], (n + -1).slot_count(1, 1) * (3 * CC * 16))
                        act.wait_ge(full[kind], n.count(1, 1))
                        for c in range(CC):
                            nc.scalar.activation(t[:, 0, c], bank_of(kind, 0)[:, c * w:(c + 1) * w], ACT.Identity,
                                                 bias=bias[:, c:c + 1]).then_inc(hi[kind], 1)

            turns(act, turn)

        @block.vector
        def _(dve):
            chain = [0]

            def link(ins):
                chain[0] += 1
                ins.then_inc(prep_done, 1)
                dve.wait_ge(prep_done, chain[0])

            dve.wait_ge(weights_in, 16 * WEIGHT_LOADS)
            nc.vector.reciprocal(temp_row[:], temp_row[:])
            link(nc.vector.reciprocal(temp_col[:], temp_col[:]))
            nc.vector.tensor_scalar_mul(temp_row[:], temp_row[:], SCALE)
            link(nc.vector.tensor_scalar_mul(temp_col[:], temp_col[:], SCALE))
            nc.vector.tensor_mul(bq_col[:], bq_col[:], temp_col[:])
            for c in range(CC):
                for m in range(CC):
                    part = raw_w[:, 0, c, m * P:(m + 1) * P].rearrange("p (d h) -> p d h", d=D)
                    last = nc.vector.tensor_tensor(part, part, temp_row[:, m * HC:(m + 1) * HC].unsqueeze(1).to_broadcast([P, D, HC]), ALU.mult)
            link(last)
            for k, w in enumerate((wq, wk, wv, wo)):
                last = nc.vector.tensor_copy(w[:, 0], raw_w[:, k])
            link(last)
            for k, w in enumerate((wq, wk, wv, wo)):
                last = nc.vector.tensor_tensor(w[:, 1], raw_w[:, k], w[:, 0].bitcast(F32), ALU.subtract)
            link(last)

            def low(kind, n, dst, src, hi_part):
                dve.wait_ge(hi[kind], n.count(1, 1))
                nc.vector.tensor_tensor(dst, src, hi_part.bitcast(F32), ALU.subtract).then_inc(emptied[kind], 1)

            def low_biased(kind, n, t, w, bias):
                dve.wait_ge(hi[kind], n.count(CC, CC))
                for c in range(CC):
                    last = nc.vector.scalar_tensor_tensor(t[:, 1, c], bank_of(kind, 0)[:, c * w:(c + 1) * w], bias[:, c:c + 1],
                                                          t[:, 0, c].bitcast(F32), ALU.add, ALU.subtract)
                last.then_inc(emptied[kind], 1)

            def norm_stats(which, src, n, stats_sem):
                for t in range(QT):
                    last = nc.vector.bn_stats(stats[:, which, t], src[:, t])
                last.then_inc(stats_sem, 1)

            def norm_var(which, n, var_sem):
                for t in range(QT):
                    last = nc.vector.bn_aggr(meanvar[:, which, t], stats[:, which, t])
                last.then_inc(var_sem, 1)

            def norm_apply(which, src, dst, n, rstd_sem, done):
                dve.wait_ge(rstd_sem, n.count(1, 1))
                for t in range(QT):
                    last = nc.vector.tensor_scalar(dst[:, t], src[:, t], meanvar[:, which, t, 0:1], rstd[:, which, t:t + 1],
                                                   ALU.subtract, ALU.mult)
                last.then_inc(done, 1)

            def flat(t):
                return t.rearrange("p c q -> p (c q)")

            def down(n, t):
                dve.wait_ge(full["down"], n.count(QT, t + 1))
                if t == 0:
                    at_least(dve, stored[n.slot], (n + -RING).slot_count(1, 2) * 16)
                nc.vector.scalar_tensor_tensor(y[:, n.slot, t], bank_of("down", t)[:, 0:C], 0.5 * DEQ * DEQ * DEQ, x1[:, n.slot, t],
                                               ALU.mult, ALU.add).then_inc(emptied["down"], 1)

            def turn(i):
                for g in range(STEPS):
                    n = i + 1
                    if n.exists(NB):
                        if g == 0:
                            at_least(dve, full["shift"], (n + -RING).count(1, 1))
                        dve.wait_ge(a_full, n.count(STEPS, g + 1))
                        qt, h0 = g * AG // H, g * AG % H
                        nc.vector.tensor_reduce(negmax[:, n.slot, qt, h0:h0 + AG], ps_a[g % 2][:, 0:AG * NKV].rearrange("p (h k) -> p h k", h=AG),
                                                AX.X, ALU.max, negate=True).then_inc(a_max, 1)
                    n = i + -2
                    if g == 0 and n.exists(NB):
                        at_least(dve, full["normT2"], (n + -1).count(1, 1))
                        norm_apply(1, x1[:, n.slot], xn2, n, rstd2, xn2_done)
                    if g == 0 and i.exists(NB):
                        low("shift", i, shiftT[:, 1], bank_of("shift", 0)[0:H, 0:NQ], shiftT[:, 0])
                    if g == 1 and n.exists(NB):
                        low("normT2", n, flat(xn2T[:, 1]), bank_of("normT2", 0)[:], flat(xn2T[:, 0]))
                    if g == 1 and (i + 2).exists(NB):
                        m = i + 2
                        dve.wait_ge(x_in[m.slot], m.slot_count(1, 1) * 16)
                        norm_stats(0, x_tok[:, m.slot], m, stats1)
                        dve.wait_ge(stats1, m.count(1, 1))
                    if g == 1 and (i + -3).exists(NB):
                        down(i + -3, 0)
                    if g == 1 and (i + 2).exists(NB):
                        norm_var(0, i + 2, var1)
                    if g == 2 and (i + -3).exists(NB):
                        down(i + -3, 1)
                    if g == 3 and (i + 2).exists(NB):
                        low("normT1", i + 2, flat(xn1T[:, 1]), bank_of("normT1", 0)[:], flat(xn1T[:, 0]))
                    if g == 5 and (i + -1).exists(NB):
                        m = i + -1
                        dve.wait_ge(pv_done, m.count(STEPS, STEPS))
                        at_least(dve, full["attT"], (m + -1).count(1, 1))
                        o = ps_o[:, :, 0:H * VW].rearrange("p t (h v) -> p t h v", v=VW)
                        nc.vector.reciprocal(rsum[:], o[:, :, :, D]).then_inc(rsum_done, 1)
                        dve.wait_ge(rsum_done, m.count(1, 1))
                        nc.vector.tensor_tensor(att[:].rearrange("p t (h d) -> p t h d", d=D), o[:, :, :, 0:D],
                                                rsum[:].unsqueeze(3).to_broadcast([P, QT, H, D]), ALU.mult).then_inc(att_done, 1)
                        low("attT", m, flat(attT[:, 1]), bank_of("attT", 0)[:], flat(attT[:, 0]))
                    if g == 6 and (i + 2).exists(NB):
                        low_biased("k", i + 2, kT, NKV, bk_col)
                    if g == 7 and (i + 2).exists(NB):
                        m = i + 2
                        if m.c == 0:
                            dve.wait_ge(consts_done, 1)
                        at_least(dve, pv_done, (m + -RING).count(STEPS, STEPS))
                        dve.wait_ge(full["v"], m.count(1, 1))
                        nc.vector.tensor_tensor(v_one[m.slot][:, :, 0:D], bank_of("v", 0)[0:NKV, 0:C].rearrange("p (h d) -> p h d", d=D),
                                                bv_row[0:NKV].rearrange("p (h d) -> p h d", d=D), ALU.add).then_inc(emptied["v"], 1)
                    if g == 7 and (i + -1).exists(NB):
                        m = i + -1
                        dve.wait_ge(full["wo"], m.count(1, 1))
                        dve.wait_ge(xres_done, m.count(1, 1))
                        if m.c == 0:
                            dve.wait_ge(gint_lo, 3)
                        nc.vector.tensor_tensor(flat(x1[:, m.slot]), bank_of("wo", 0)[:], flat(x_res[:, m.slot]), ALU.add).then_inc(emptied["wo"], 1)
                        dve.wait_ge(emptied["wo"], m.count(1, 1))
                        norm_stats(1, x1[:, m.slot], m, stats2)
                        dve.wait_ge(stats2, m.count(1, 1))
                    if g >= 2 and n.exists(NB):
                        f = g - 2
                        ps = bank_of("gateup", f)
                        at_least(dve, hid_lo, n.count(FC, f - 1))
                        dve.wait_ge(tanh_done, n.count(FC, f + 1))
                        nc.vector.scalar_tensor_tensor(hid[:, f % 2], tanh_g[:, f % 2], 1.0, ps[:, 0:NQ], ALU.add, ALU.mult).then_inc(gated_done, 1)
                        dve.wait_ge(gated_done, n.count(FC, f + 1))
                        nc.vector.tensor_tensor(hid[:, f % 2], hid[:, f % 2], ps[:, NQ:2 * NQ], ALU.mult).then_inc(emptied["gateup"], 1)
                    if g == 7 and (i + -1).exists(NB):
                        norm_var(1, i + -1, var2)
                    if g == 2 and (i + 2).exists(NB):
                        at_least(dve, full["normT1"], (i + 1).count(1, 1))
                        norm_apply(0, x_tok[:, (i + 2).slot], xn1, i + 2, rstd1, xn1_done)
                    if g == 4 and (i + 2).exists(NB):
                        low_biased("q", i + 2, qT, NQ, bq_col)

            turns(dve, turn)

        @block.tensor
        def _(pe):
            PARTS = [(0, 0), (1, 0), (0, 1)]

            pe.wait_ge(ident_done, 2)
            pe.wait_ge(prep_done, 5)

            def product(dst, pairs):
                for k, (lhsT, rhs) in enumerate(pairs):
                    last = nc.tensor.matmul(dst, lhsT, rhs, start=(k == 0), stop=(k == len(pairs) - 1))
                return last

            def transposes(ps, src):
                for c in range(CC):
                    for t in range(QT):
                        last = nc.tensor.transpose(ps[:, c * NQ + t * P:c * NQ + (t + 1) * P], src[:, t, c * P:(c + 1) * P], ident[:])
                return last

            def job(kind, idx, n, ps):
                if kind == "shift":
                    pe.wait_ge(a_max, n.count(STEPS, STEPS))
                    for t in range(QT):
                        last = nc.tensor.transpose(ps[0:H, t * P:(t + 1) * P], negmax[:, n.slot, t], ident[:])
                elif kind == "normT1":
                    pe.wait_ge(xn1_done, n.count(1, 1))
                    last = transposes(ps, xn1)
                elif kind == "normT2":
                    pe.wait_ge(xn2_done, n.count(1, 1))
                    last = transposes(ps, xn2)
                elif kind == "attT":
                    pe.wait_ge(att_done, n.count(1, 1))
                    last = transposes(ps, att)
                elif kind == "q":
                    pe.wait_ge(emptied["normT1"], n.count(1, 1))
                    for m in range(CC):
                        last = product(ps[:, m * NQ:(m + 1) * NQ],
                                       [(wq[:, a, c, m * P:(m + 1) * P], xn1T[:, b, c]) for a, b in PARTS for c in range(CC)])
                elif kind == "k":
                    pe.wait_ge(ctx_lo, n.count(1, 1))
                    for m in range(CC):
                        last = product(ps[:, m * NKV:(m + 1) * NKV],
                                       [(wk[:, a, c, m * P:(m + 1) * P], ctxT[:, b, c]) for a, b in PARTS for c in range(CC)])
                elif kind == "v":
                    last = product(ps[0:NKV, 0:C], [(ctxT[:, a, c], wv[:, b, c]) for a, b in PARTS for c in range(CC)])
                elif kind == "wo":
                    pe.wait_ge(emptied["attT"], n.count(1, 1))
                    for t in range(QT):
                        last = product(ps[:, t * C:(t + 1) * C],
                                       [(attT[:, a, c, t * P:(t + 1) * P], wo[:, b, c]) for a, b in PARTS for c in range(CC)])
                elif kind == "gateup":
                    if idx == 0:
                        pe.wait_ge(emptied["normT2"], n.count(1, 1))
                        if n.c == 0:
                            pe.wait_ge(gint_lo, 2)
                    for k, w in enumerate((wg, wu)):
                        last = product(ps[:, k * NQ:(k + 1) * NQ],
                                       [(w[:, a, c, idx * P:(idx + 1) * P], xn2T[:, b, c]) for a, b in PARTS for c in range(CC)])
                elif kind == "down":
                    if idx == 0:
                        pe.wait_ge(hid_lo, n.count(FC, FC))
                        if n.c == 0:
                            pe.wait_ge(gint_lo, 3)
                    last = product(ps[:, 0:C], [(hidT[:, a, f, idx * P:(idx + 1) * P], wd[:, b, f]) for a, b in PARTS for f in range(FC)])
                last.then_inc(full[kind], 1)

            def turn(i):
                for g in range(STEPS):
                    n = i + 1
                    if n.exists(NB):
                        if g == 0:
                            pe.wait_ge(qs_in[n.slot], n.slot_count(1, 1) * (3 * CC * 16))
                            pe.wait_ge(ks_in[n.slot], n.slot_count(1, 1) * (3 * CC * 16))
                        at_least(pe, a_max, n.count(STEPS, g - 1))
                        qt, h0 = g * AG // H, g * AG % H
                        for k in range(AG):
                            last = nc.tensor.matmul(ps_a[g % 2][:, k * NKV:(k + 1) * NKV], qs[n.slot][0:KS_ROWS, h0 + k, qt * P:(qt + 1) * P],
                                                    ks[n.slot][0:KS_ROWS, h0 + k], start=True, stop=True)
                        last.then_inc(a_full, 1)
                    n, gb = second_pass(i, g)
                    if n.exists(NB):
                        if gb == 0:
                            pe.wait_ge(shift_in[n.slot], n.slot_count(1, 1) * 32)
                        at_least(pe, exp_done, n.count(STEPS, gb - 1))
                        for k in range(HG):
                            last = nc.tensor.matmul(ps_b[gb % 2][0:NKV, k * NQ:(k + 1) * NQ], ks[n.slot][:, gb * HG + k], qs[n.slot][:, gb * HG + k],
                                                    start=True, stop=True)
                        last.then_inc(b_full, 1)
                    for pos, (step, kind, idx, off) in enumerate(JOBS):
                        if step == g and (i + off).exists(NB):
                            before = job_before(pos, i)
                            if before:
                                pe.wait_ge(emptied[before[0]], job_count(*before))
                            job(kind, idx, i + off, ps_w[pos % 2])
                    n, gb = (n, gb - 1) if gb else (n + -1, STEPS - 1)
                    if n.exists(NB):
                        pe.wait_ge(exp_done, n.count(STEPS, gb + 1))
                        if gb == 0:
                            pe.wait_ge(emptied["v"], n.count(1, 1))
                            at_least(pe, att_done, (n + -1).count(1, 1))
                        for k in range(HG):
                            h = gb * HG + k
                            for t in range(QT):
                                last = nc.tensor.matmul(ps_o[:, t, h * VW:(h + 1) * VW], probs[0:NKV, gb % 4, k * NQ + t * P:k * NQ + (t + 1) * P],
                                                        v_one[n.slot][:, h], start=True, stop=True)
                        last.then_inc(pv_done, 1)

            turns(pe, turn)


_ORDER = ["x", "ctx", "wqT", "bq", "wkT", "bk", "wvT", "bv", "woT", "bo", "temp", "tempc", "wgT", "wuT", "wdT"]


def kernel(**inputs):
    import numpy as np
    import concourse.bacc as bacc
    from concourse.bass_utils import run_bass_kernel_spmd as run

    a = {k.replace("L0_xattn_", "").replace("L0_ffn_", ""): np.asarray(v) for k, v in inputs.items()}
    heads = a["temperature"].size
    d = a["Wq"].shape[0] // heads

    def by_depth(v):
        return v.reshape(*v.shape[:-1], -1, P // d, d).swapaxes(-1, -2).reshape(v.shape)

    def chunks(v):
        return by_depth(v).reshape(-1, P).T

    data = {
        "x": a["x"], "ctx": a["ctx_1024"].transpose(0, 2, 1),
        "wqT": by_depth(a["Wq"].T), "bq": chunks(a["bq"]), "wkT": by_depth(a["Wk"].T), "bk": chunks(a["bk"]), "wvT": a["Wv"].T, "bv": a["bv"],
        "woT": a["Wo"].T, "bo": a["bo"], "temp": a["temperature"],
        "tempc": chunks(np.repeat(a["temperature"], d)),
        "wgT": a["w_gate"].T, "wuT": a["w_up"].T, "wdT": a["w_down"].T,
    }
    data = {k: np.ascontiguousarray(v) for k, v in data.items()}
    nc = bacc.Bacc("TRN2", target_bir_lowering=False, num_devices=1)
    args = [nc.dram_tensor(k, data[k].shape, mybir.dt.from_np(data[k].dtype), kind="ExternalInput").ap() for k in _ORDER]
    y = nc.dram_tensor("out", data["x"].shape, F32, kind="ExternalOutput").ap()
    build(nc, *args, y)
    r = run(nc, [data], core_ids=[0])
    return r.results[0]["out"]
```

```python
import concourse.bass as bass
from concourse import mybir
from contextlib import ExitStack

F32 = mybir.dt.float32
F32R = mybir.dt.float32r
BF16 = mybir.dt.bfloat16
I32 = mybir.dt.int32
ALU = mybir.AluOpType
ACT = mybir.ActivationFunctionType
AX = mybir.AxisListType

P = 128
RING = 3
FIRST, LAST = -3, 18
LOOP_FROM, LOOP_TURNS = 4, 3

JOBS = [
    (0, "shift", 0, 0),
    (1, "normT1", 0, 2), (1, "normT2", 0, -2), (1, "down", 0, -3),
    (2, "down", 1, -3), (2, "gateup", 0, -2), (2, "q", 0, 2),
    (3, "gateup", 1, -2), (3, "k", 0, 2),
    (4, "gateup", 2, -2), (4, "v", 0, 2),
    (5, "attQ", 0, -1), (5, "attQ", 1, -1), (5, "gateup", 3, -2),
    (6, "attT", 0, -1), (6, "gateup", 4, -2),
    (7, "wo", 0, -1), (7, "gateup", 5, -2),
]
STEPS = 8


class Batch:

    def __init__(self, loop, c):
        self.loop, self.c = loop, c

    def __add__(self, d):
        return Batch(self.loop, self.c + d)

    @property
    def slot(self):
        return self.c % RING

    def exists(self, n_batches):
        return self.loop is not None or 0 <= self.c < n_batches

    def count(self, per, k):
        c = self.c * per + k
        assert self.loop is None or c > 0, (self.c, per, k)
        return c if self.loop is None else self.loop * (RING * per) + c

    def slot_count(self, per, k):
        c = (self.c // RING) * per + k
        assert self.loop is None or c > 0, (self.c, per, k)
        return c if self.loop is None else self.loop * per + c

    def number(self):
        return self.c if self.loop is None else self.loop * RING + self.c


def at_least(eng, sem, value):
    if not (isinstance(value, int) and value <= 0):
        eng.wait_ge(sem, value)


def turns(eng, turn):
    for c in range(FIRST, LOOP_FROM):
        turn(Batch(None, c))
    with eng.Fori(0, LOOP_TURNS) as j:
        for u in range(RING):
            turn(Batch(j, LOOP_FROM + u))
    for c in range(LOOP_FROM + RING * LOOP_TURNS, LAST + 1):
        turn(Batch(None, c))


def build(nc, x, ctx, wqT, bq, wkT, bk, wvT, bv, woT, bo, temp, tempc, wgT, wuT, wdT, out):
    NB, NQ, C = x.shape
    NKV = ctx.shape[2]
    H = temp.shape[0]
    D = C // H
    HID = wgT.shape[1]
    CC = C // P
    QT = NQ // P
    HC = H // CC
    FC = HID // P
    VW = 2 * D
    HQ = 4
    SCALE = float(D) ** -0.5
    EPS = 1e-5
    DEQ = 1.0 / 127.0
    HG = 2
    AG = H * QT // STEPS
    WEIGHT_LOADS = 4 + 6
    Q_PARTS = (0, 1, 0, 2, 0, 1)
    K_PARTS = (0, 0, 1, 0, 2, 1)
    KS_ROWS = len(Q_PARTS) * D
    assert CC == 2 and QT == 2 and H * 16 == C and FC == 6 and NB == 16
    assert H == HG * STEPS and AG * NKV <= 512

    es = ExitStack()
    with es:
        def sb(name, shape, dt=F32):
            return es.enter_context(nc.sbuf_tensor(name, shape, dt))

        def psum(name, shape):
            return es.enter_context(nc.psum_tensor(name, shape, F32))

        def sem(name):
            return es.enter_context(nc.semaphore(name))

        wq = sb("wq", [P, 2, CC, C], F32R)
        wk = sb("wk", [P, 2, CC, C], F32R)
        wv = sb("wv", [P, 2, CC, C], F32R)
        wo = sb("wo", [P, 2, CC, C], F32R)
        wg = sb("wg", [P, 2, CC, HID], F32R)
        wu = sb("wu", [P, 2, CC, HID], F32R)
        wd = sb("wd", [P, 2, FC, C], F32R)
        temp_row = sb("temp_row", [P, H])
        temp_col = sb("temp_col", [P, CC])
        bq_col = sb("bq_col", [P, CC])
        bk_col = sb("bk_col", [P, CC])
        bv_row = sb("bv_row", [P, C])
        bo_row = sb("bo_row", [P, C])
        ident = sb("ident", [P, P])
        minus_half = sb("minus_half", [P, QT])
        eps_col = sb("eps_col", [P, QT])

        x_tok = sb("x_tok", [P, RING, QT, C])
        x_res = sb("x_res", [P, RING, QT, C])
        ctx_raw = sb("ctx_raw", [P, RING, CC, NKV])
        ctxT = sb("ctxT", [P, 2, CC, NKV], F32R)
        stats = sb("stats", [P, 2, QT, 6])
        meanvar = sb("meanvar", [P, 2, QT, 2])
        vareps = sb("vareps", [P, 2, QT])
        rstd = sb("rstd", [P, 2, QT])
        xn1 = sb("xn1", [P, QT, C])
        xn2 = sb("xn2", [P, QT, C])
        xn1T = sb("xn1T", [P, 2, CC, NQ], F32R)
        xn2T = sb("xn2T", [P, 2, CC, NQ], F32R)
        q3 = sb("q3", [P, 3, CC, NQ], BF16)
        k3 = sb("k3", [P, 3, CC, NKV], BF16)
        q_rest = sb("q_rest", [P, CC, NQ])
        k_rest = sb("k_rest", [P, CC, NKV])
        qs = [sb(f"qs{r}", [KS_ROWS + 2, H, NQ], BF16) for r in range(RING)]
        ks = [sb(f"ks{r}", [KS_ROWS + 2, H, NKV], BF16) for r in range(RING)]
        v_one = [sb(f"v_one{r}", [NKV, H, VW]) for r in range(RING)]
        negmax = sb("negmax", [P, RING, QT, H])
        shiftT = sb("shiftT", [H, 2, NQ], BF16)
        probs = sb("probs", [P, 4, HG * NQ])
        pv_T = sb("pv_T", [P, H // HQ, NQ])
        rsum = sb("rsum", [P, QT, H])
        att = sb("att", [P, QT, C])
        attT = sb("attT", [P, 2, CC, NQ], F32R)
        x1 = sb("x1", [P, RING, QT, C])
        tanh_g = sb("tanh_g", [P, 2, NQ])
        hid = sb("hid", [P, 2, NQ])
        hidT = sb("hidT", [P, 2, FC, NQ], F32R)
        y = sb("y", [P, RING, QT, C])
        raw_w = probs[:].rearrange("p a (b c) -> p a b c", c=C)
        raw_i = y[:].bitcast(I32).rearrange("p r t c -> p (r t c)")
        raw_f = x1[:].rearrange("p r t c -> p (r t c)")

        ps_a = [psum(f"ps_a{b}", [P, 512]) for b in range(2)]
        ps_b = [psum(f"ps_b{b}", [P, 512]) for b in range(2)]
        ps_o = psum("ps_o", [P, H // HQ, NQ])
        ps_w = [psum(f"ps_w{b}", [P, 512]) for b in range(2)]

        weights_in = sem("weights_in")
        gate_in, up_in, down_in = sem("gate_in"), sem("up_in"), sem("down_in")
        x_in = [sem(f"x_in{r}") for r in range(RING)]
        xres_in = [sem(f"xres_in{r}") for r in range(RING)]
        ctx_in = [sem(f"ctx_in{r}") for r in range(RING)]
        qs_in = [sem(f"qs_in{r}") for r in range(RING)]
        ks_in = [sem(f"ks_in{r}") for r in range(RING)]
        shift_in = [sem(f"shift_in{r}") for r in range(RING)]
        stored = [sem(f"stored{r}") for r in range(RING)]
        consts_done = sem("consts_done")
        ident_done = sem("ident_done")
        prep_done = sem("prep_done")
        gint_f, gint_hi, gint_lo = sem("gint_f"), sem("gint_hi"), sem("gint_lo")
        full = {k: sem(f"{k}_full") for k in ("shift", "normT2", "down", "gateup", "normT1", "q", "attQ", "attT", "k", "v", "wo")}
        a_full, b_full, pv_done = sem("a_full"), sem("b_full"), sem("pv_done")
        hi = {k: sem(f"{k}_hi") for k in ("shift", "normT2", "normT1", "q", "attT", "k", "ctx", "hid")}
        mid = {k: sem(f"{k}_mid") for k in ("q", "k")}
        pv_copied = sem("pv_copied")
        exp_done, tanh_done = sem("exp_done"), sem("tanh_done")
        emptied = {k: sem(f"{k}_emptied") for k in ("shift", "normT2", "down", "gateup", "normT1", "q", "attQ", "attT", "k", "v", "wo")}
        a_max, rsum_done = sem("a_max"), sem("rsum_done")
        stats1, stats2 = sem("stats1"), sem("stats2")
        var1, var2 = sem("var1"), sem("var2")
        xn1_done, xn2_done = sem("xn1_done"), sem("xn2_done")
        gated_done = sem("gated_done")
        eps1, eps2 = sem("eps1"), sem("eps2")
        rstd1, rstd2 = sem("rstd1"), sem("rstd2")
        ctx_lo, hid_lo, xres_done = sem("ctx_lo"), sem("hid_lo"), sem("xres_done")
        lowest = {k: sem(f"{k}_lowest") for k in ("q", "k")}

        per_batch = {"gateup": FC, "down": QT, "attQ": QT}
        PV = H // HQ

        def job_count(kind, idx, n):
            return n.count(per_batch.get(kind, 1), idx + 1)

        def job_before(pos, i):
            back = 0
            while True:
                pos -= 2
                if pos < 0:
                    pos, back = pos + len(JOBS), back + 1
                if (i + -back).c < FIRST - 1:
                    return None
                _, kind, idx, off = JOBS[pos]
                n = i + (off - back)
                if n.exists(NB):
                    return kind, idx, n

        def bank_of(kind, idx):
            return next(ps_w[pos % 2] for pos, (_, k, x_, _) in enumerate(JOBS) if (k, x_) == (kind, idx))

        def second_pass(i, g):
            return (i, g - 4) if g >= 4 else (i + -1, g + 4)

        block = es.enter_context(nc.Block())

        @block.sync
        def _(sp):
            def row(v):
                return v.rearrange("(a n) -> a n", a=1)

            for k, w in enumerate((wqT, wkT, wvT, woT)):
                sp.dma_start(raw_w[:, k], w.rearrange("(c p) n -> p c n", p=P)).then_inc(weights_in, 16)
            small = [
                (temp_row[:], temp.rearrange("h a b -> (a b) h").to_broadcast([P, H])),
                (bv_row[:], row(bv).to_broadcast([P, C])),
                (bo_row[:], row(bo).to_broadcast([P, C])),
                (bq_col[:], bq),
                (bk_col[:], bk),
                (temp_col[:], tempc),
            ]
            for dst, src in small:
                sp.dma_start(dst, src).then_inc(weights_in, 16)
            def turn(i):
                n = i + 3
                if n.exists(NB):
                    at_least(sp, xn1_done, (n + -RING).count(1, 1))
                    sp.dma_start(x_tok[:, n.slot], x[n.number()].rearrange("(t p) c -> p t c", p=P)).then_inc(x_in[n.slot], 16)
                    at_least(sp, ctx_lo, (n + -RING).count(1, 1))
                    sp.dma_start(ctx_raw[:, n.slot], ctx[n.number()].rearrange("(c p) k -> p c k", p=P)).then_inc(ctx_in[n.slot], 16)
                n = i
                if n.exists(NB):
                    at_least(sp, emptied["wo"], (n + -RING).count(1, 1))
                    sp.dma_start(x_res[:, n.slot], x[n.number()].rearrange("(t p) c -> p t c", p=P)).then_inc(xres_in[n.slot], 16)
                    sp.wait_ge(emptied["shift"], n.count(1, 1))
                    for part in range(2):
                        sp.dma_start(qs[n.slot][KS_ROWS + part:KS_ROWS + part + 1], shiftT[:, part]).then_inc(shift_in[n.slot], 16)
                n = i + -3
                if n.exists(NB):
                    sp.wait_ge(emptied["down"], n.count(QT, QT))
                    sp.dma_start(out[n.number()].rearrange("(t p) c -> p t c", p=P), y[:, n.slot]).then_inc(stored[n.slot], 16)
                n = i + 2
                if n.exists(NB):
                    for kind, t, stack, arrived, parts in (("q", q3, qs, qs_in, Q_PARTS), ("k", k3, ks, ks_in, K_PARTS)):
                        at_least(sp, b_full, (n + -RING).count(STEPS, STEPS))
                        sp.wait_ge(lowest[kind], n.count(1, 1))
                        for r, part in enumerate(parts):
                            sp.dma_start(stack[n.slot][r * D:(r + 1) * D], t[:, part]).then_inc(arrived[n.slot], 16)

            for r in range(RING):
                sp.sem_inc(stored[r], 16)
            turns(sp, turn)
            for r in range(RING):
                sp.wait_ge(stored[r], 16 * (1 + len(range(r, NB, RING))))

        @block.gpsimd
        def _(pool):
            nc.gpsimd.memset(ident[:], 0.0).then_inc(ident_done, 1)
            pool.wait_ge(ident_done, 1)
            nc.gpsimd.affine_select(out=ident[:], in_=ident[:], compare_op=ALU.not_equal, fill=1.0, base=0,
                                    pattern=[[-1, P]], channel_multiplier=1).then_inc(ident_done, 1)
            nc.gpsimd.memset(minus_half[:], -0.5)
            nc.gpsimd.memset(eps_col[:], EPS)
            for r in range(RING):
                nc.gpsimd.memset(v_one[r][:], 1.0)
                last = nc.gpsimd.memset(ks[r][:], 1.0)
            last.then_inc(consts_done, 1)
            pool.wait_ge(consts_done, 1)

            def integer_weight_lo(k, w):
                pool.wait_ge(gint_hi, k + 1)
                flat = w[:, 1].rearrange("p c n -> p (c n)")
                nc.gpsimd.tensor_tensor(flat, raw_f, w[:, 0].bitcast(F32).rearrange("p c n -> p (c n)"),
                                        ALU.subtract).then_inc(gint_lo, 1)

            def rsqrt(which, n, got, eps_sem, out_sem):
                pool.wait_ge(got, n.count(1, 1))
                nc.gpsimd.tensor_tensor(vareps[:, which], meanvar[:, which, :, 1], eps_col[:], ALU.add).then_inc(eps_sem, 1)
                pool.wait_ge(eps_sem, n.count(1, 1))
                nc.gpsimd.tensor_tensor(rstd[:, which], vareps[:, which], minus_half[:], ALU.pow).then_inc(out_sem, 1)

            def hidden_lo(n, f):
                pool.wait_ge(hi["hid"], n.count(FC, f + 1))
                nc.gpsimd.tensor_tensor(hidT[:, 1, f], hid[:, f % 2], hidT[:, 0, f].bitcast(F32), ALU.subtract).then_inc(hid_lo, 1)

            def third(kind, n, t, rest):
                pool.wait_ge(mid[kind], n.count(1, 1))
                nc.gpsimd.tensor_tensor(t[:, 2], rest[:], t[:, 1], ALU.subtract).then_inc(lowest[kind], 1)

            def turn(i):
                if i.loop is None and FIRST <= i.c < FIRST + 3:
                    integer_weight_lo(i.c - FIRST, (wg, wu, wd)[i.c - FIRST])
                if (i + -3).exists(NB):
                    hidden_lo(i + -3, FC - 1)
                n = i + 2
                if n.exists(NB):
                    pool.wait_ge(hi["ctx"], n.count(1, 1))
                    nc.gpsimd.tensor_tensor(ctxT[:, 1], ctx_raw[:, n.slot], ctxT[:, 0].bitcast(F32), ALU.subtract).then_inc(ctx_lo, 1)
                n = i
                if n.exists(NB):
                    pool.wait_ge(xres_in[n.slot], n.slot_count(1, 1) * 16)
                    if n.c == 0:
                        pool.wait_ge(weights_in, 16 * WEIGHT_LOADS)
                    for t in range(QT):
                        last = nc.gpsimd.tensor_tensor(x_res[:, n.slot, t], x_res[:, n.slot, t], bo_row[:], ALU.add)
                    last.then_inc(xres_done, 1)
                if (i + -2).exists(NB):
                    hidden_lo(i + -2, 0)
                if (i + 2).exists(NB):
                    third("q", i + 2, q3, q_rest)
                if (i + -2).exists(NB):
                    hidden_lo(i + -2, 1)
                if (i + 2).exists(NB):
                    third("k", i + 2, k3, k_rest)
                if (i + -2).exists(NB):
                    hidden_lo(i + -2, 2)
                    hidden_lo(i + -2, 3)
                if (i + 3).exists(NB):
                    rsqrt(0, i + 3, var1, eps1, rstd1)
                if (i + -2).exists(NB):
                    hidden_lo(i + -2, 4)
                if (i + -1).exists(NB):
                    rsqrt(1, i + -1, var2, eps2, rstd2)

            turns(pool, turn)

        @block.scalar
        def _(act):
            act.dma_start(raw_i.rearrange("p (c n) -> p c n", c=CC), wgT.rearrange("(c p) n -> p c n", p=P)).then_inc(gate_in, 16)

            def integer_weight(k):
                arrived, w = ((gate_in, wg), (up_in, wu), (down_in, wd))[k]
                act.wait_ge(arrived, 16)
                at_least(act, gint_lo, k)
                nc.scalar.activation(raw_f, raw_i, ACT.Copy).then_inc(gint_f, 1)
                act.wait_ge(gint_f, k + 1)
                nc.scalar.activation(w[:, 0].rearrange("p c n -> p (c n)"), raw_f, ACT.Copy).then_inc(gint_hi, 1)
                if k == 0:
                    act.dma_start(raw_i.rearrange("p (c n) -> p c n", c=CC), wuT.rearrange("(c p) n -> p c n", p=P)).then_inc(up_in, 16)
                if k == 1:
                    act.dma_start(raw_i.rearrange("p (c n) -> p c n", c=FC), wdT.rearrange("(c p) n -> p c n", p=P)).then_inc(down_in, 16)

            def high(kind, n, dst, src):
                act.wait_ge(full[kind], n.count(1, 1))
                nc.scalar.activation(dst, src, ACT.Copy).then_inc(hi[kind], 1)

            def hidden_hi(n, f):
                if f == 0:
                    at_least(act, full["down"], (n + -1).count(QT, QT))
                act.wait_ge(emptied["gateup"], n.count(FC, f + 1))
                nc.scalar.activation(hidT[:, 0, f], hid[:, f % 2], ACT.Copy).then_inc(hi["hid"], 1)

            def turn(i):
                if i.loop is None and FIRST <= i.c < FIRST + 3:
                    integer_weight(i.c - FIRST)
                for g in range(STEPS):
                    n, gb = second_pass(i, g)
                    if n.exists(NB):
                        if gb % 2 == 0:
                            at_least(act, pv_done, n.count(PV, gb // 2 - 1))
                        act.wait_ge(b_full, n.count(STEPS, gb + 1))
                        nc.scalar.activation(probs[0:NKV, gb % 4], ps_b[gb % 2][0:NKV], ACT.Exp).then_inc(exp_done, 1)
                    if g == 0:
                        if (i + -3).exists(NB):
                            hidden_hi(i + -3, FC - 1)
                        if i.exists(NB):
                            if i.loop is not None or i.c > 0:
                                act.wait_ge(shift_in[(i + -1).slot], (i + -1).slot_count(1, 1) * 32)
                            act.wait_ge(full["shift"], i.count(1, 1))
                            nc.scalar.activation(shiftT[:, 0], bank_of("shift", 0)[0:H, 0:NQ], ACT.Copy).then_inc(hi["shift"], 1)
                    if g == 0 and (i + 2).exists(NB):
                        n = i + 2
                        act.wait_ge(ctx_in[n.slot], n.slot_count(1, 1) * 16)
                        at_least(act, full["v"], (n + -1).count(1, 1))
                        nc.scalar.activation(ctxT[:, 0], ctx_raw[:, n.slot], ACT.Copy).then_inc(hi["ctx"], 1)
                    if g == 1 and (i + 2).exists(NB):
                        at_least(act, full["q"], (i + 1).count(1, 1))
                        high("normT1", i + 2, xn1T[:, 0].rearrange("p c q -> p (c q)"), bank_of("normT1", 0)[:])
                    if g == 1 and (i + -2).exists(NB):
                        at_least(act, full["gateup"], (i + -3).count(FC, FC))
                        high("normT2", i + -2, xn2T[:, 0].rearrange("p c q -> p (c q)"), bank_of("normT2", 0)[:])
                    if g == 5 and (i + -1).exists(NB):
                        at_least(act, full["attQ"], (i + -2).count(QT, QT))
                        act.wait_ge(pv_done, (i + -1).count(PV, PV))
                        nc.scalar.activation(pv_T[:], ps_o[:], ACT.Copy).then_inc(pv_copied, 1)
                    if g == 6 and (i + -1).exists(NB):
                        at_least(act, full["wo"], (i + -2).count(1, 1))
                        high("attT", i + -1, attT[:, 0].rearrange("p c q -> p (c q)"), bank_of("attT", 0)[:])
                    n = i + -2
                    if g >= 2 and n.exists(NB):
                        f = g - 2
                        act.wait_ge(full["gateup"], n.count(FC, f + 1))
                        at_least(act, gated_done, n.count(FC, f - 1))
                        nc.scalar.activation(tanh_g[:, f % 2], bank_of("gateup", f)[:, 0:NQ], ACT.Tanh, scale=DEQ / 2).then_inc(tanh_done, 1)
                        if f >= 1:
                            hidden_hi(n, f - 1)
                    n = i + 2
                    if (g == 2 or g == 3) and n.exists(NB):
                        kind, t, w, bias, arrived = ("q", q3, NQ, bq_col, qs_in) if g == 2 else ("k", k3, NKV, bk_col, ks_in)
                        if n.loop is not None or n.c > 0:
                            act.wait_ge(arrived[(n + -1).slot], (n + -1).slot_count(1, 1) * (6 * 16))
                        act.wait_ge(full[kind], n.count(1, 1))
                        for c in range(CC):
                            nc.scalar.activation(t[:, 0, c], bank_of(kind, 0)[:, c * w:(c + 1) * w], ACT.Identity,
                                                 bias=bias[:, c:c + 1]).then_inc(hi[kind], 1)
                    if (g == 3 or g == 4) and n.exists(NB):
                        kind, t, rest = ("q", q3, q_rest) if g == 3 else ("k", k3, k_rest)
                        act.wait_ge(emptied[kind], n.count(1, 1))
                        nc.scalar.activation(t[:, 1], rest[:], ACT.Copy).then_inc(mid[kind], 1)

            turns(act, turn)

        @block.vector
        def _(dve):
            chain = [0]

            def link(ins):
                chain[0] += 1
                ins.then_inc(prep_done, 1)
                dve.wait_ge(prep_done, chain[0])

            dve.wait_ge(weights_in, 16 * WEIGHT_LOADS)
            nc.vector.reciprocal(temp_row[:], temp_row[:])
            link(nc.vector.reciprocal(temp_col[:], temp_col[:]))
            nc.vector.tensor_scalar_mul(temp_row[:], temp_row[:], SCALE)
            link(nc.vector.tensor_scalar_mul(temp_col[:], temp_col[:], SCALE))
            nc.vector.tensor_mul(bq_col[:], bq_col[:], temp_col[:])
            for c in range(CC):
                for m in range(CC):
                    part = raw_w[:, 0, c, m * P:(m + 1) * P].rearrange("p (d h) -> p d h", d=D)
                    last = nc.vector.tensor_tensor(part, part, temp_row[:, m * HC:(m + 1) * HC].unsqueeze(1).to_broadcast([P, D, HC]), ALU.mult)
            link(last)
            for k, w in enumerate((wq, wk, wv, wo)):
                last = nc.vector.tensor_copy(w[:, 0], raw_w[:, k])
            link(last)
            for k, w in enumerate((wq, wk, wv, wo)):
                last = nc.vector.tensor_tensor(w[:, 1], raw_w[:, k], w[:, 0].bitcast(F32), ALU.subtract)
            link(last)

            def low(kind, n, dst, src, hi_part):
                dve.wait_ge(hi[kind], n.count(1, 1))
                nc.vector.tensor_tensor(dst, src, hi_part, ALU.subtract).then_inc(emptied[kind], 1)

            def rest_of(kind, n, t, rest, w, bias):
                at_least(dve, lowest[kind], (n + -1).count(1, 1))
                dve.wait_ge(hi[kind], n.count(CC, CC))
                for c in range(CC):
                    last = nc.vector.scalar_tensor_tensor(rest[:, c], bank_of(kind, 0)[:, c * w:(c + 1) * w], bias[:, c:c + 1],
                                                          t[:, 0, c], ALU.add, ALU.subtract)
                last.then_inc(emptied[kind], 1)

            def norm_stats(which, src, n, stats_sem):
                for t in range(QT):
                    last = nc.vector.bn_stats(stats[:, which, t], src[:, t])
                last.then_inc(stats_sem, 1)

            def norm_var(which, n, var_sem):
                for t in range(QT):
                    last = nc.vector.bn_aggr(meanvar[:, which, t], stats[:, which, t])
                last.then_inc(var_sem, 1)

            def norm_apply(which, src, dst, n, rstd_sem, done):
                dve.wait_ge(rstd_sem, n.count(1, 1))
                for t in range(QT):
                    last = nc.vector.tensor_scalar(dst[:, t], src[:, t], meanvar[:, which, t, 0:1], rstd[:, which, t:t + 1],
                                                   ALU.subtract, ALU.mult)
                last.then_inc(done, 1)

            def flat(t):
                return t.rearrange("p c q -> p (c q)")

            def down(n, t):
                dve.wait_ge(full["down"], n.count(QT, t + 1))
                if t == 0:
                    at_least(dve, stored[n.slot], (n + -RING).slot_count(1, 2) * 16)
                nc.vector.scalar_tensor_tensor(y[:, n.slot, t], bank_of("down", t)[:, 0:C], 0.5 * DEQ * DEQ * DEQ, x1[:, n.slot, t],
                                               ALU.mult, ALU.add).then_inc(emptied["down"], 1)

            def turn(i):
                for g in range(STEPS):
                    n = i + 1
                    if n.exists(NB):
                        if g == 0:
                            at_least(dve, full["shift"], (n + -RING).count(1, 1))
                        dve.wait_ge(a_full, n.count(STEPS, g + 1))
                        qt, h0 = g * AG // H, g * AG % H
                        nc.vector.tensor_reduce(negmax[:, n.slot, qt, h0:h0 + AG], ps_a[g % 2][:, 0:AG * NKV].rearrange("p (h k) -> p h k", h=AG),
                                                AX.X, ALU.max, negate=True).then_inc(a_max, 1)
                    if g == 0 and (i + 2).exists(NB):
                        at_least(dve, full["normT1"], (i + 1).count(1, 1))
                        norm_apply(0, x_tok[:, (i + 2).slot], xn1, i + 2, rstd1, xn1_done)
                    if g == 0 and (i + -2).exists(NB):
                        at_least(dve, full["normT2"], (i + -3).count(1, 1))
                        norm_apply(1, x1[:, (i + -2).slot], xn2, i + -2, rstd2, xn2_done)
                    if g == 0 and i.exists(NB):
                        low("shift", i, shiftT[:, 1], bank_of("shift", 0)[0:H, 0:NQ], shiftT[:, 0])
                    if g == 1 and (i + 2).exists(NB):
                        low("normT1", i + 2, flat(xn1T[:, 1]), bank_of("normT1", 0)[:], flat(xn1T[:, 0]).bitcast(F32))
                    if g == 1 and (i + -2).exists(NB):
                        low("normT2", i + -2, flat(xn2T[:, 1]), bank_of("normT2", 0)[:], flat(xn2T[:, 0]).bitcast(F32))
                    if g == 1 and (i + -3).exists(NB):
                        down(i + -3, 0)
                    if g == 2 and (i + -3).exists(NB):
                        down(i + -3, 1)
                    if g == 3 and (i + 2).exists(NB):
                        rest_of("q", i + 2, q3, q_rest, NQ, bq_col)
                    if g == 4 and (i + 2).exists(NB):
                        rest_of("k", i + 2, k3, k_rest, NKV, bk_col)
                    if g == 5 and (i + 2).exists(NB):
                        m = i + 2
                        if m.c == 0:
                            dve.wait_ge(consts_done, 1)
                        at_least(dve, pv_done, (m + -RING).count(PV, PV))
                        dve.wait_ge(full["v"], m.count(1, 1))
                        nc.vector.tensor_tensor(v_one[m.slot][:, :, 0:D], bank_of("v", 0)[0:NKV, 0:C].rearrange("p (h d) -> p h d", d=D),
                                                bv_row[0:NKV].rearrange("p (h d) -> p h d", d=D), ALU.add).then_inc(emptied["v"], 1)
                    if g == 5 and (i + -1).exists(NB):
                        m = i + -1
                        at_least(dve, full["attT"], (m + -1).count(1, 1))
                        for t in range(QT):
                            o = bank_of("attQ", t)[:].rearrange("p (h v) -> p h v", v=VW)
                            dve.wait_ge(full["attQ"], m.count(QT, t + 1))
                            nc.vector.reciprocal(rsum[:, t], o[:, :, D]).then_inc(rsum_done, 1)
                            dve.wait_ge(rsum_done, m.count(QT, t + 1))
                            nc.vector.tensor_tensor(att[:, t].rearrange("p (h d) -> p h d", d=D), o[:, :, 0:D],
                                                    rsum[:, t].unsqueeze(2).to_broadcast([P, H, D]), ALU.mult).then_inc(emptied["attQ"], 1)
                    if g == 6 and (i + -1).exists(NB):
                        low("attT", i + -1, flat(attT[:, 1]), bank_of("attT", 0)[:], flat(attT[:, 0]).bitcast(F32))
                    if g == 6 and (i + 3).exists(NB):
                        m = i + 3
                        dve.wait_ge(x_in[m.slot], m.slot_count(1, 1) * 16)
                        norm_stats(0, x_tok[:, m.slot], m, stats1)
                        dve.wait_ge(stats1, m.count(1, 1))
                    if g == 7 and (i + -1).exists(NB):
                        m = i + -1
                        dve.wait_ge(full["wo"], m.count(1, 1))
                        dve.wait_ge(xres_done, m.count(1, 1))
                        if m.c == 0:
                            dve.wait_ge(gint_lo, 3)
                        nc.vector.tensor_tensor(flat(x1[:, m.slot]), bank_of("wo", 0)[:], flat(x_res[:, m.slot]), ALU.add).then_inc(emptied["wo"], 1)
                        dve.wait_ge(emptied["wo"], m.count(1, 1))
                        norm_stats(1, x1[:, m.slot], m, stats2)
                        dve.wait_ge(stats2, m.count(1, 1))
                    n = i + -2
                    if g >= 2 and n.exists(NB):
                        f = g - 2
                        ps = bank_of("gateup", f)
                        at_least(dve, hid_lo, n.count(FC, f - 1))
                        dve.wait_ge(tanh_done, n.count(FC, f + 1))
                        nc.vector.scalar_tensor_tensor(hid[:, f % 2], tanh_g[:, f % 2], 1.0, ps[:, 0:NQ], ALU.add, ALU.mult).then_inc(gated_done, 1)
                        dve.wait_ge(gated_done, n.count(FC, f + 1))
                        nc.vector.tensor_tensor(hid[:, f % 2], hid[:, f % 2], ps[:, NQ:2 * NQ], ALU.mult).then_inc(emptied["gateup"], 1)
                    if g == 6 and (i + 3).exists(NB):
                        norm_var(0, i + 3, var1)
                    if g == 7 and (i + -1).exists(NB):
                        norm_var(1, i + -1, var2)

            turns(dve, turn)

        @block.tensor
        def _(pe):
            PARTS = [(0, 0), (1, 0), (0, 1)]

            pe.wait_ge(ident_done, 2)
            pe.wait_ge(prep_done, 5)

            def product(dst, pairs):
                for k, (lhsT, rhs) in enumerate(pairs):
                    last = nc.tensor.matmul(dst, lhsT, rhs, start=(k == 0), stop=(k == len(pairs) - 1))
                return last

            def transposes(ps, src):
                for c in range(CC):
                    for t in range(QT):
                        last = nc.tensor.transpose(ps[:, c * NQ + t * P:c * NQ + (t + 1) * P], src[:, t, c * P:(c + 1) * P], ident[:])
                return last

            def job(kind, idx, n, ps):
                if kind == "shift":
                    pe.wait_ge(a_max, n.count(STEPS, STEPS))
                    for t in range(QT):
                        last = nc.tensor.transpose(ps[0:H, t * P:(t + 1) * P], negmax[:, n.slot, t], ident[:])
                elif kind == "normT1":
                    pe.wait_ge(xn1_done, n.count(1, 1))
                    last = transposes(ps, xn1)
                elif kind == "normT2":
                    pe.wait_ge(xn2_done, n.count(1, 1))
                    last = transposes(ps, xn2)
                elif kind == "attT":
                    pe.wait_ge(emptied["attQ"], n.count(QT, QT))
                    last = transposes(ps, att)
                elif kind == "attQ":
                    if idx == 0:
                        pe.wait_ge(pv_copied, n.count(1, 1))
                    for k in range(PV):
                        last = nc.tensor.transpose(ps[:, k * P:(k + 1) * P], pv_T[:, k, idx * P:(idx + 1) * P], ident[:])
                elif kind == "q":
                    pe.wait_ge(emptied["normT1"], n.count(1, 1))
                    for m in range(CC):
                        last = product(ps[:, m * NQ:(m + 1) * NQ],
                                       [(wq[:, a, c, m * P:(m + 1) * P], xn1T[:, b, c]) for a, b in PARTS for c in range(CC)])
                elif kind == "k":
                    pe.wait_ge(ctx_lo, n.count(1, 1))
                    for m in range(CC):
                        last = product(ps[:, m * NKV:(m + 1) * NKV],
                                       [(wk[:, a, c, m * P:(m + 1) * P], ctxT[:, b, c]) for a, b in PARTS for c in range(CC)])
                elif kind == "v":
                    last = product(ps[0:NKV, 0:C], [(ctxT[:, a, c], wv[:, b, c]) for a, b in PARTS for c in range(CC)])
                elif kind == "wo":
                    pe.wait_ge(emptied["attT"], n.count(1, 1))
                    for t in range(QT):
                        last = product(ps[:, t * C:(t + 1) * C],
                                       [(attT[:, a, c, t * P:(t + 1) * P], wo[:, b, c]) for a, b in PARTS for c in range(CC)])
                elif kind == "gateup":
                    if idx == 0:
                        pe.wait_ge(emptied["normT2"], n.count(1, 1))
                        if n.c == 0:
                            pe.wait_ge(gint_lo, 2)
                    for k, w in enumerate((wg, wu)):
                        last = product(ps[:, k * NQ:(k + 1) * NQ],
                                       [(w[:, a, c, idx * P:(idx + 1) * P], xn2T[:, b, c]) for a, b in PARTS for c in range(CC)])
                elif kind == "down":
                    if idx == 0:
                        pe.wait_ge(hid_lo, n.count(FC, FC))
                        if n.c == 0:
                            pe.wait_ge(gint_lo, 3)
                    last = product(ps[:, 0:C], [(hidT[:, a, f, idx * P:(idx + 1) * P], wd[:, b, f]) for a, b in PARTS for f in range(FC)])
                last.then_inc(full[kind], 1)

            def turn(i):
                for g in range(STEPS):
                    n = i + 1
                    if n.exists(NB):
                        if g == 0:
                            pe.wait_ge(qs_in[n.slot], n.slot_count(1, 1) * (6 * 16))
                            pe.wait_ge(ks_in[n.slot], n.slot_count(1, 1) * (6 * 16))
                        at_least(pe, a_max, n.count(STEPS, g - 1))
                        qt, h0 = g * AG // H, g * AG % H
                        for k in range(AG):
                            last = nc.tensor.matmul(ps_a[g % 2][:, k * NKV:(k + 1) * NKV], qs[n.slot][0:KS_ROWS, h0 + k, qt * P:(qt + 1) * P],
                                                    ks[n.slot][0:KS_ROWS, h0 + k], start=True, stop=True)
                        last.then_inc(a_full, 1)
                    n, gb = second_pass(i, g)
                    if n.exists(NB):
                        if gb == 0:
                            pe.wait_ge(shift_in[n.slot], n.slot_count(1, 1) * 32)
                        at_least(pe, exp_done, n.count(STEPS, gb - 1))
                        for k in range(HG):
                            last = nc.tensor.matmul(ps_b[gb % 2][0:NKV, k * NQ:(k + 1) * NQ], ks[n.slot][:, gb * HG + k], qs[n.slot][:, gb * HG + k],
                                                    start=True, stop=True)
                        last.then_inc(b_full, 1)
                    for pos, (step, kind, idx, off) in enumerate(JOBS):
                        if step == g and (i + off).exists(NB):
                            before = job_before(pos, i)
                            if before:
                                pe.wait_ge(emptied[before[0]], job_count(*before))
                            job(kind, idx, i + off, ps_w[pos % 2])
                    n, gb = (n, gb - 1) if gb else (n + -1, STEPS - 1)
                    if gb % 2 and n.exists(NB):
                        pe.wait_ge(exp_done, n.count(STEPS, gb + 1))
                        if gb == 1:
                            pe.wait_ge(emptied["v"], n.count(1, 1))
                            at_least(pe, pv_copied, (n + -1).count(1, 1))
                        for k in range(HQ):
                            last = nc.tensor.matmul(ps_o[k * VW:(k + 1) * VW, gb // 2], v_one[n.slot][:, gb // 2 * HQ + k],
                                                    probs[0:NKV, (gb - 1 + k // HG) % 4, k % HG * NQ:(k % HG + 1) * NQ], start=True, stop=True)
                        last.then_inc(pv_done, 1)

            turns(pe, turn)


_ORDER = ["x", "ctx", "wqT", "bq", "wkT", "bk", "wvT", "bv", "woT", "bo", "temp", "tempc", "wgT", "wuT", "wdT"]


def kernel(**inputs):
    import numpy as np
    import concourse.bacc as bacc
    from concourse.bass_utils import run_bass_kernel_spmd as run

    a = {k.replace("L0_xattn_", "").replace("L0_ffn_", ""): np.asarray(v) for k, v in inputs.items()}
    heads = a["temperature"].size
    d = a["Wq"].shape[0] // heads

    def by_depth(v):
        return v.reshape(*v.shape[:-1], -1, P // d, d).swapaxes(-1, -2).reshape(v.shape)

    def chunks(v):
        return by_depth(v).reshape(-1, P).T

    def head_order(v):
        return v.reshape(-1, P // d, d, *v.shape[1:]).swapaxes(0, 1).reshape(v.shape)

    data = {
        "x": a["x"], "ctx": a["ctx_1024"].transpose(0, 2, 1),
        "wqT": by_depth(a["Wq"].T), "bq": chunks(a["bq"]), "wkT": by_depth(a["Wk"].T), "bk": chunks(a["bk"]), "wvT": head_order(a["Wv"]).T, "bv": head_order(a["bv"]),
        "woT": head_order(a["Wo"].T), "bo": a["bo"], "temp": a["temperature"],
        "tempc": chunks(np.repeat(a["temperature"], d)),
        "wgT": a["w_gate"].T, "wuT": a["w_up"].T, "wdT": a["w_down"].T,
    }
    data = {k: np.ascontiguousarray(v) for k, v in data.items()}
    nc = bacc.Bacc("TRN2", target_bir_lowering=False, num_devices=1)
    args = [nc.dram_tensor(k, data[k].shape, mybir.dt.from_np(data[k].dtype), kind="ExternalInput").ap() for k in _ORDER]
    y = nc.dram_tensor("out", data["x"].shape, F32, kind="ExternalOutput").ap()
    build(nc, *args, y)
    r = run(nc, [data], core_ids=[0])
    return r.results[0]["out"]
```

```python
import concourse.bass as bass
from concourse import mybir
from contextlib import ExitStack

F32 = mybir.dt.float32
F32R = mybir.dt.float32r
BF16 = mybir.dt.bfloat16
I32 = mybir.dt.int32
ALU = mybir.AluOpType
ACT = mybir.ActivationFunctionType
AX = mybir.AxisListType

P = 128
RING = 3
FIRST, LAST = -3, 18
LOOP_FROM, LOOP_TURNS = 4, 3

JOBS = [
    (0, "k", 0, 2, 0), (0, "gateup", 3, -3, 1), (0, "normT1", 0, 2, 2),
    (1, "wo", 0, -2, 0), (1, "gateup", 4, -3, 1), (1, "shift", 0, 0, 2),
    (2, "gateup", 5, -3, 0),
    (3, "q", 0, 2, 1), (3, "v", 0, 2, 2),
    (4, "down", 0, -3, 3), (4, "normT2", 0, -2, 0),
    (5, "down", 1, -3, 1), (5, "gateup", 0, -2, 2),
    (6, "attQ", 0, -1, 3), (6, "attQ", 1, -1, 0), (6, "gateup", 1, -2, 1),
    (7, "gateup", 2, -2, 2), (7, "attT", 0, -1, 3),
]
STEPS = 8


class Batch:

    def __init__(self, loop, c):
        self.loop, self.c = loop, c

    def __add__(self, d):
        return Batch(self.loop, self.c + d)

    @property
    def slot(self):
        return self.c % RING

    def exists(self, n_batches):
        return self.loop is not None or 0 <= self.c < n_batches

    def count(self, per, k):
        c = self.c * per + k
        assert self.loop is None or c > 0, (self.c, per, k)
        return c if self.loop is None else self.loop * (RING * per) + c

    def slot_count(self, per, k):
        c = (self.c // RING) * per + k
        assert self.loop is None or c > 0, (self.c, per, k)
        return c if self.loop is None else self.loop * per + c

    def number(self):
        return self.c if self.loop is None else self.loop * RING + self.c


def at_least(eng, sem, value):
    if not (isinstance(value, int) and value <= 0):
        eng.wait_ge(sem, value)


def turns(eng, turn):
    for c in range(FIRST, LOOP_FROM):
        turn(Batch(None, c))
    with eng.Fori(0, LOOP_TURNS) as j:
        for u in range(RING):
            turn(Batch(j, LOOP_FROM + u))
    for c in range(LOOP_FROM + RING * LOOP_TURNS, LAST + 1):
        turn(Batch(None, c))


def build(nc, x, ctx, wqT, bq, wkT, bk, wvT, bv, woT, bo, temp, tempc, wgT, wuT, wdT, out):
    NB, NQ, C = x.shape
    NKV = ctx.shape[2]
    H = temp.shape[0]
    D = C // H
    HID = wgT.shape[1]
    CC = C // P
    QT = NQ // P
    HC = H // CC
    FC = HID // P
    VW = 2 * D
    HQ = 4
    SCALE = float(D) ** -0.5
    EPS = 1e-5
    DEQ = 1.0 / 127.0
    HG = 2
    AG = H * QT // STEPS
    Q_PARTS = (0, 1, 0, 2, 0, 1)
    K_PARTS = (0, 0, 1, 0, 2, 1)
    KS_ROWS = len(Q_PARTS) * D
    assert CC == 2 and QT == 2 and H * 16 == C and FC == 6 and NB == 16
    assert H == HG * STEPS and AG * NKV <= 512

    es = ExitStack()
    with es:
        def sb(name, shape, dt=F32):
            return es.enter_context(nc.sbuf_tensor(name, shape, dt))

        def psum(name, shape):
            return es.enter_context(nc.psum_tensor(name, shape, F32))

        def sem(name):
            return es.enter_context(nc.semaphore(name))

        wq = sb("wq", [P, 2, CC, C], F32R)
        wk = sb("wk", [P, 2, CC, C], F32R)
        wv = sb("wv", [P, 2, CC, C], F32R)
        wo = sb("wo", [P, 2, CC, C], F32R)
        wg = sb("wg", [P, 2, CC, HID], F32R)
        wu = sb("wu", [P, 2, CC, HID], F32R)
        wd = sb("wd", [P, 2, FC, C], F32R)
        temp_row = sb("temp_row", [P, H])
        temp_col = sb("temp_col", [P, CC])
        bq_col = sb("bq_col", [P, CC])
        bk_col = sb("bk_col", [P, CC])
        bv_row = sb("bv_row", [P, C])
        bo_row = sb("bo_row", [P, C])
        ident = sb("ident", [P, P])
        wide_max = sb("wide_max", [P, 3])
        wide_any = sb("wide_any", [P, 1])
        ones_col = sb("ones_col", [P, 1])
        wide_int = sb("wide_int", [1, 1], I32)
        minus_half = sb("minus_half", [P, QT])
        eps_col = sb("eps_col", [P, QT])
        zero_col = sb("zero_col", [P, QT])

        x_tok = sb("x_tok", [P, RING, QT, C])
        x_res = sb("x_res", [P, RING, QT, C])
        ctx_raw = sb("ctx_raw", [P, RING, CC, NKV])
        ctxT = sb("ctxT", [P, 2, CC, NKV], F32R)
        stats = sb("stats", [P, 2, QT, 6])
        meanvar = sb("meanvar", [P, 2, QT, 2])
        vareps = sb("vareps", [P, 2, QT])
        minus_mean = sb("minus_mean", [P, 2, QT])
        norm_bias = sb("norm_bias", [P, 2, QT])
        rstd = sb("rstd", [P, 2, QT])
        xn1 = sb("xn1", [P, QT, C])
        xn2 = sb("xn2", [P, QT, C])
        xn1T = sb("xn1T", [P, 2, CC, NQ], F32R)
        xn2T = sb("xn2T", [P, 2, CC, NQ], F32R)
        q3 = sb("q3", [P, 3, CC, NQ], BF16)
        k3 = sb("k3", [P, 3, CC, NKV], BF16)
        q_rest = sb("q_rest", [P, CC, NQ])
        k_rest = sb("k_rest", [P, CC, NKV])
        qs = [sb(f"qs{r}", [KS_ROWS + 2, H, NQ], BF16) for r in range(RING)]
        ks = [sb(f"ks{r}", [KS_ROWS + 2, H, NKV], BF16) for r in range(RING)]
        v_one = [sb(f"v_one{r}", [NKV, H, VW]) for r in range(RING)]
        negmax = sb("negmax", [P, RING, QT, H])
        shiftT = sb("shiftT", [H, 2, NQ], BF16)
        probs = sb("probs", [P, 4, HG * NQ])
        pv_T = sb("pv_T", [P, H // HQ, NQ])
        rsum = sb("rsum", [P, QT, H])
        att = sb("att", [P, QT, C])
        attT = sb("attT", [P, 2, CC, NQ], F32R)
        x1 = sb("x1", [P, RING, QT, C])
        tanh_g = sb("tanh_g", [P, 2, NQ])
        hid = sb("hid", [P, 2, NQ])
        hidT = sb("hidT", [P, 2, FC, NQ], F32R)
        y = sb("y", [P, RING, QT, C])
        raw_w = probs[:].rearrange("p a (b c) -> p a b c", c=C)
        raw_i = y[:].bitcast(I32).rearrange("p r t c -> p (r t c)")
        raw_f = x1[:].rearrange("p r t c -> p (r t c)")

        ps_a = psum("ps_a", [P, 512])
        ps_b = psum("ps_b", [P, 512])
        ps_o = psum("ps_o", [P, H // HQ, NQ])
        ps_w = [psum(f"ps_w{b}", [P, 512]) for b in range(4)]

        weight_in = {k: sem(f"w{k}_in") for k in "kqvo"}
        bk_in, temp_in, bias_in = sem("bk_in"), sem("temp_in"), sem("bias_in")
        gate_in, up_in, down_in = sem("gate_in"), sem("up_in"), sem("down_in")
        x_in = [sem(f"x_in{r}") for r in range(RING)]
        xres_in = [sem(f"xres_in{r}") for r in range(RING)]
        ctx_in = [sem(f"ctx_in{r}") for r in range(RING)]
        qs_in = [sem(f"qs_in{r}") for r in range(RING)]
        ks_in = [sem(f"ks_in{r}") for r in range(RING)]
        shift_in = [sem(f"shift_in{r}") for r in range(RING)]
        stored = [sem(f"stored{r}") for r in range(RING)]
        consts_done = sem("consts_done")
        ident_done = sem("ident_done")
        temp_step = sem("temp_step")
        k_ones_set, v_ones_set = sem("k_ones_set"), sem("v_ones_set")
        w_ready = {k: sem(f"w{k}_ready") for k in "kqvo"}
        wide_got, wide_col, wide_sum, wide_set = sem("wide_got"), sem("wide_col"), sem("wide_sum"), sem("wide_set")
        gint_f, gint_hi, gint_lo = sem("gint_f"), sem("gint_hi"), sem("gint_lo")
        full = {k: sem(f"{k}_full") for k in ("shift", "normT2", "down", "gateup", "normT1", "q", "attQ", "attT", "k", "v", "wo")}
        a_full, b_full, pv_done = sem("a_full"), sem("b_full"), sem("pv_done")
        hi = {k: sem(f"{k}_hi") for k in ("shift", "normT2", "normT1", "q", "attT", "k", "ctx", "hid")}
        mid = {k: sem(f"{k}_mid") for k in ("q", "k")}
        xn1_done, xn2_done = sem("xn1_done"), sem("xn2_done")
        pv_copied = sem("pv_copied")
        exp_done, tanh_done = sem("exp_done"), sem("tanh_done")
        emptied = {k: sem(f"{k}_emptied") for k in ("shift", "normT2", "down", "gateup", "normT1", "q", "attQ", "attT", "k", "v", "wo")}
        a_max, rsum_done = sem("a_max"), sem("rsum_done")
        stats1, stats2 = sem("stats1"), sem("stats2")
        var1, var2 = sem("var1"), sem("var2")
        gated_done = sem("gated_done")
        hid_lo_last = sem("hid_lo_last")
        eps1, eps2 = sem("eps1"), sem("eps2")
        rstd1, rstd2 = sem("rstd1"), sem("rstd2")
        norm1, norm2 = sem("norm1"), sem("norm2")
        ctx_lo, hid_lo, xres_done = sem("ctx_lo"), sem("hid_lo"), sem("xres_done")
        lowest = {k: sem(f"{k}_lowest") for k in ("q", "k")}

        per_batch = {"gateup": FC, "down": QT, "attQ": QT}
        PV = H // HQ

        def job_count(kind, idx, n):
            return n.count(per_batch.get(kind, 1), idx + 1)

        def job_before(pos, i):
            bank, back = JOBS[pos][4], 0
            while True:
                pos -= 1
                if pos < 0:
                    pos, back = pos + len(JOBS), back + 1
                if (i + -back).c < FIRST - 1:
                    return None
                _, kind, idx, off, its_bank = JOBS[pos]
                n = i + (off - back)
                if its_bank == bank and n.exists(NB):
                    return kind, idx, n

        def bank_of(kind, idx):
            return next(ps_w[bank] for _, k, x_, _, bank in JOBS if (k, x_) == (kind, idx))

        def hidden_chunk(i, g):
            return (i + -2, g - 5) if g >= 5 else (i + -3, g + 3) if g <= 2 else (None, 0)

        def wait_hidden_lo(eng, n, f):
            if f < 0:
                n, f = n + -1, f + FC
            if f == FC - 1:
                at_least(eng, hid_lo_last, n.count(1, 1))
            else:
                at_least(eng, hid_lo, n.count(FC - 1, f + 1))

        def first_pass(i, g):
            return (i + 1, g - 2) if g >= 2 else (i, g + 6)

        def second_pass(i, g):
            return (i, g - 4) if g >= 4 else (i + -1, g + 4)

        block = es.enter_context(nc.Block())

        @block.sync
        def _(sp):
            def row(v):
                return v.rearrange("(a n) -> a n", a=1)

            def load_weight(k, w):
                sp.dma_start(raw_w[:, "kqvo".index(k)], w.rearrange("(c p) n -> p c n", p=P)).then_inc(weight_in[k], 16)

            def load_x_and_ctx(n):
                at_least(sp, ctx_lo, (n + -RING).count(1, 1))
                sp.dma_start(ctx_raw[:, n.slot], ctx[n.number()].rearrange("(c p) k -> p c k", p=P)).then_inc(ctx_in[n.slot], 16)
                at_least(sp, xn1_done, (n + -RING).count(1, 1))
                sp.dma_start(x_tok[:, n.slot], x[n.number()].rearrange("(t p) c -> p t c", p=P)).then_inc(x_in[n.slot], 16)

            load_weight("k", wkT)
            load_x_and_ctx(Batch(None, 0))
            sp.dma_start(bk_col[:], bk).then_inc(bk_in, 16)
            sp.dma_start(temp_row[:], temp.rearrange("h a b -> (a b) h").to_broadcast([P, H])).then_inc(temp_in, 16)
            sp.dma_start(temp_col[:], tempc).then_inc(temp_in, 16)
            sp.dma_start(bq_col[:], bq).then_inc(temp_in, 16)
            load_weight("q", wqT)
            sp.dma_start(bv_row[:], row(bv).to_broadcast([P, C])).then_inc(bias_in, 16)
            sp.dma_start(bo_row[:], row(bo).to_broadcast([P, C])).then_inc(bias_in, 16)
            load_weight("v", wvT)
            load_weight("o", woT)

            def stack(kind, n, t, dst, arrived, parts):
                if kind == "k":
                    at_least(sp, b_full, (n + -RING).count(STEPS, STEPS))
                for part, ready in enumerate((hi, mid, lowest)):
                    sp.wait_ge(ready[kind], n.count(1, 1))
                    for r in range(len(parts)):
                        if parts[r] == part:
                            sp.dma_start(dst[n.slot][r * D:(r + 1) * D], t[:, part]).then_inc(arrived[n.slot], 16)

            def turn(i):
                n = i + 3
                if n.exists(NB) and (n.loop is not None or n.c > 0):
                    load_x_and_ctx(n)
                if i.exists(NB):
                    sp.wait_ge(emptied["shift"], i.count(1, 1))
                    for part in range(2):
                        sp.dma_start(qs[i.slot][KS_ROWS + part:KS_ROWS + part + 1], shiftT[:, part]).then_inc(shift_in[i.slot], 16)
                if (i + 2).exists(NB):
                    stack("k", i + 2, k3, ks, ks_in, K_PARTS)
                if i.exists(NB):
                    at_least(sp, emptied["wo"], (i + -RING).count(1, 1))
                    sp.dma_start(x_res[:, i.slot], x[i.number()].rearrange("(t p) c -> p t c", p=P)).then_inc(xres_in[i.slot], 16)
                if (i + 2).exists(NB):
                    stack("q", i + 2, q3, qs, qs_in, Q_PARTS)
                n = i + -3
                if n.exists(NB):
                    sp.wait_ge(emptied["down"], n.count(QT, QT))
                    sp.dma_start(out[n.number()].rearrange("(t p) c -> p t c", p=P), y[:, n.slot]).then_inc(stored[n.slot], 16)

            for r in range(RING):
                sp.sem_inc(stored[r], 16)
            turns(sp, turn)
            for r in range(RING):
                sp.wait_ge(stored[r], 16 * (1 + len(range(r, NB, RING))))

        @block.gpsimd
        def _(pool):
            nc.gpsimd.memset(ident[:], 0.0).then_inc(ident_done, 1)
            pool.wait_ge(ident_done, 1)
            nc.gpsimd.affine_select(out=ident[:], in_=ident[:], compare_op=ALU.not_equal, fill=1.0, base=0,
                                    pattern=[[-1, P]], channel_multiplier=1).then_inc(ident_done, 1)
            nc.gpsimd.memset(minus_half[:], -0.5)
            nc.gpsimd.memset(eps_col[:], EPS)
            nc.gpsimd.memset(zero_col[:], 0.0)
            nc.gpsimd.memset(ones_col[:], 1.0).then_inc(consts_done, 1)
            pool.wait_ge(consts_done, 1)

            def integer_weight_lo(k, w):
                pool.wait_ge(gint_hi, k + 1)
                flat = w[:, 1].rearrange("p c n -> p (c n)")
                nc.gpsimd.tensor_tensor(flat, raw_f, w[:, 0].bitcast(F32).rearrange("p c n -> p (c n)"),
                                        ALU.subtract).then_inc(gint_lo, 1)

            def rsqrt(which, n, got, eps_sem, out_sem, norm_sem):
                pool.wait_ge(got, n.count(1, 1))
                nc.gpsimd.tensor_tensor(minus_mean[:, which], zero_col[:], meanvar[:, which, :, 0], ALU.subtract)
                nc.gpsimd.tensor_tensor(vareps[:, which], meanvar[:, which, :, 1], eps_col[:], ALU.add).then_inc(eps_sem, 1)
                pool.wait_ge(eps_sem, n.count(1, 1))
                nc.gpsimd.tensor_tensor(rstd[:, which], vareps[:, which], minus_half[:], ALU.pow).then_inc(out_sem, 1)
                pool.wait_ge(out_sem, n.count(1, 1))
                nc.gpsimd.tensor_tensor(norm_bias[:, which], minus_mean[:, which], rstd[:, which], ALU.mult).then_inc(norm_sem, 1)

            def hidden_lo(n, f):
                pool.wait_ge(hi["hid"], n.count(FC, f + 1))
                nc.gpsimd.tensor_tensor(hidT[:, 1, f], hid[:, f % 2], hidT[:, 0, f].bitcast(F32), ALU.subtract).then_inc(hid_lo, 1)

            def third(kind, n, t, rest):
                pool.wait_ge(mid[kind], n.count(1, 1))
                nc.gpsimd.tensor_tensor(t[:, 2], rest[:], t[:, 1], ALU.subtract).then_inc(lowest[kind], 1)

            def turn(i):
                if i.loop is None and i.c == FIRST + 1:
                    pool.wait_ge(norm1, 1)
                    for r in range(RING):
                        last = nc.gpsimd.memset(ks[r][KS_ROWS:], 1.0)
                    last.then_inc(k_ones_set, 1)
                    pool.wait_ge(k_ones_set, 1)
                early, late, ahead = i + -3, i + -2, i + 2
                if early.exists(NB):
                    hidden_lo(early, 2)
                if ahead.exists(NB):
                    third("k", ahead, k3, k_rest)
                if early.exists(NB):
                    hidden_lo(early, 3)
                    hidden_lo(early, 4)
                if late.exists(NB):
                    rsqrt(1, late, var2, eps2, rstd2, norm2)
                if ahead.exists(NB):
                    third("q", ahead, q3, q_rest)
                n = i + 3
                if n.exists(NB):
                    pool.wait_ge(hi["ctx"], n.count(1, 1))
                    nc.gpsimd.tensor_tensor(ctxT[:, 1], ctx_raw[:, n.slot], ctxT[:, 0].bitcast(F32), ALU.subtract).then_inc(ctx_lo, 1)
                if i.exists(NB):
                    pool.wait_ge(xres_in[i.slot], i.slot_count(1, 1) * 16)
                    if i.c == 0:
                        pool.wait_ge(bias_in, 16 * 2)
                    for t in range(QT):
                        last = nc.gpsimd.tensor_tensor(x_res[:, i.slot, t], x_res[:, i.slot, t], bo_row[:], ALU.add)
                    last.then_inc(xres_done, 1)
                if n.exists(NB):
                    rsqrt(0, n, var1, eps1, rstd1, norm1)
                if late.exists(NB):
                    hidden_lo(late, 0)
                    hidden_lo(late, 1)
                if i.loop is None and -2 <= i.c <= 0:
                    integer_weight_lo(i.c + 2, (wg, wu, wd)[i.c + 2])

            turns(pool, turn)

        @block.scalar
        def _(act):
            def integer_weight(k):
                arrived, w = ((gate_in, wg), (up_in, wu), (down_in, wd))[k]
                act.wait_ge(arrived, 16)
                at_least(act, gint_lo, k)
                nc.scalar.activation(raw_f, raw_i, ACT.Copy).then_inc(gint_f, 1)
                act.wait_ge(gint_f, k + 1)
                nc.scalar.activation(w[:, 0].rearrange("p c n -> p (c n)"), raw_f, ACT.Copy).then_inc(gint_hi, 1)
                if k == 0:
                    act.dma_start(raw_i.rearrange("p (c n) -> p c n", c=CC), wuT.rearrange("(c p) n -> p c n", p=P)).then_inc(up_in, 16)
                if k == 1:
                    act.dma_start(raw_i.rearrange("p (c n) -> p c n", c=FC), wdT.rearrange("(c p) n -> p c n", p=P)).then_inc(down_in, 16)

            def high(kind, n, dst, src):
                act.wait_ge(full[kind], n.count(1, 1))
                nc.scalar.activation(dst, src, ACT.Copy).then_inc(hi[kind], 1)

            def highest(kind, n, t, w, bias, arrived):
                if n.loop is not None or n.c > 0:
                    act.wait_ge(arrived[(n + -1).slot], (n + -1).slot_count(1, 1) * (6 * 16))
                if kind == "k" and n.c == 0:
                    act.wait_ge(bk_in, 16)
                act.wait_ge(full[kind], n.count(1, 1))
                for c in range(CC):
                    last = nc.scalar.activation(t[:, 0, c], bank_of(kind, 0)[:, c * w:(c + 1) * w], ACT.Identity, bias=bias[:, c:c + 1])
                last.then_inc(hi[kind], 1)

            def middle(kind, n, t, rest):
                act.wait_ge(emptied[kind], n.count(1, 1))
                nc.scalar.activation(t[:, 1], rest[:], ACT.Copy).then_inc(mid[kind], 1)

            def norm_apply(which, src, dst, n, norm_sem, done):
                act.wait_ge(norm_sem, n.count(1, 1))
                for t in range(QT):
                    last = nc.scalar.activation(dst[:, t], src[:, t], ACT.Identity, bias=norm_bias[:, which, t:t + 1], scale=rstd[:, which, t:t + 1])
                last.then_inc(done, 1)

            def hidden_hi(n, f):
                if f == 0:
                    at_least(act, full["down"], (n + -1).count(QT, QT))
                act.wait_ge(emptied["gateup"], n.count(FC, f + 1))
                nc.scalar.activation(hidT[:, 0, f], hid[:, f % 2], ACT.Copy).then_inc(hi["hid"], 1)

            def turn(i):
                for g in range(STEPS):
                    n, gb = second_pass(i, g)
                    if n.exists(NB):
                        if gb % 2 == 0:
                            at_least(act, pv_done, n.count(PV, gb // 2 - 1))
                        act.wait_ge(b_full, n.count(STEPS, gb + 1))
                        nc.scalar.activation(probs[0:NKV, gb % 4], ps_b[0:NKV], ACT.Exp).then_inc(exp_done, 1)
                    if g == 0 and (i + 2).exists(NB):
                        highest("k", i + 2, k3, NKV, bk_col, ks_in)
                    if g == 5 and (i + -1).exists(NB):
                        at_least(act, full["attQ"], (i + -2).count(QT, QT))
                        act.wait_ge(pv_done, (i + -1).count(PV, PV))
                        nc.scalar.activation(pv_T[:], ps_o[:], ACT.Copy).then_inc(pv_copied, 1)
                    n, f = hidden_chunk(i, g)
                    if n and n.exists(NB):
                        act.wait_ge(full["gateup"], n.count(FC, f + 1))
                        at_least(act, gated_done, n.count(FC, f - 1))
                        nc.scalar.activation(tanh_g[:, f % 2], bank_of("gateup", f)[:, 0:NQ], ACT.Tanh, scale=DEQ / 2).then_inc(tanh_done, 1)
                    if g == 1 and i.exists(NB):
                        if i.loop is not None or i.c > 0:
                            act.wait_ge(shift_in[(i + -1).slot], (i + -1).slot_count(1, 1) * 32)
                        act.wait_ge(full["shift"], i.count(1, 1))
                        nc.scalar.activation(shiftT[:, 0], bank_of("shift", 0)[0:H, 0:NQ], ACT.Copy).then_inc(hi["shift"], 1)
                    n, f = hidden_chunk(i, g - 1) if g else hidden_chunk(i + -1, STEPS - 1)
                    if n and n.exists(NB):
                        hidden_hi(n, f)
                    if g == 3 and (i + 2).exists(NB):
                        highest("q", i + 2, q3, NQ, bq_col, qs_in)
                    if g == 3 and (i + -2).exists(NB):
                        at_least(act, full["normT2"], (i + -3).count(1, 1))
                        norm_apply(1, x1[:, (i + -2).slot], xn2, i + -2, norm2, xn2_done)
                    if g == 0 and (i + 2).exists(NB):
                        at_least(act, full["q"], (i + 1).count(1, 1))
                        high("normT1", i + 2, xn1T[:, 0].rearrange("p c q -> p (c q)"), bank_of("normT1", 0)[:])
                    if g == 1 and (i + 2).exists(NB):
                        middle("k", i + 2, k3, k_rest)
                    if g == 4 and (i + 2).exists(NB):
                        middle("q", i + 2, q3, q_rest)
                    if g == 4 and (i + -2).exists(NB):
                        at_least(act, full["gateup"], (i + -3).count(FC, FC))
                        high("normT2", i + -2, xn2T[:, 0].rearrange("p c q -> p (c q)"), bank_of("normT2", 0)[:])
                    n = i + 3
                    if g == 4 and n.exists(NB):
                        act.wait_ge(ctx_in[n.slot], n.slot_count(1, 1) * 16)
                        at_least(act, full["v"], (n + -1).count(1, 1))
                        nc.scalar.activation(ctxT[:, 0], ctx_raw[:, n.slot], ACT.Copy).then_inc(hi["ctx"], 1)
                    if g == 7 and (i + 3).exists(NB):
                        at_least(act, full["normT1"], (i + 2).count(1, 1))
                        norm_apply(0, x_tok[:, (i + 3).slot], xn1, i + 3, norm1, xn1_done)
                    if g == 7 and (i + -1).exists(NB):
                        at_least(act, full["wo"], (i + -2).count(1, 1))
                        high("attT", i + -1, attT[:, 0].rearrange("p c q -> p (c q)"), bank_of("attT", 0)[:])
                if i.loop is None and i.c == FIRST:
                    act.dma_start(raw_i.rearrange("p (c n) -> p c n", c=CC), wgT.rearrange("(c p) n -> p c n", p=P)).then_inc(gate_in, 16)
                if i.loop is None and -2 <= i.c <= 0:
                    integer_weight(i.c + 2)

            turns(act, turn)

        @block.vector
        def _(dve):
            def split_weight(k, w):
                raw = raw_w[:, "kqvo".index(k)]
                nc.vector.tensor_copy(w[:, 0], raw).then_inc(w_ready[k], 1)
                dve.wait_ge(w_ready[k], 1)
                nc.vector.tensor_tensor(w[:, 1], raw, w[:, 0].bitcast(F32), ALU.subtract).then_inc(w_ready[k], 1)

            def scale_query_weight():
                dve.wait_ge(temp_in, 16 * 3)
                nc.vector.reciprocal(temp_row[:], temp_row[:])
                nc.vector.reciprocal(temp_col[:], temp_col[:]).then_inc(temp_step, 1)
                dve.wait_ge(temp_step, 1)
                nc.vector.tensor_scalar_mul(temp_row[:], temp_row[:], SCALE)
                nc.vector.tensor_scalar_mul(temp_col[:], temp_col[:], SCALE).then_inc(temp_step, 1)
                dve.wait_ge(temp_step, 2)
                nc.vector.tensor_mul(bq_col[:], bq_col[:], temp_col[:])
                dve.wait_ge(weight_in["q"], 16)
                for c in range(CC):
                    for m in range(CC):
                        part = raw_w[:, "kqvo".index("q"), c, m * P:(m + 1) * P].rearrange("p (d h) -> p d h", d=D)
                        last = nc.vector.tensor_tensor(part, part, temp_row[:, m * HC:(m + 1) * HC].unsqueeze(1).to_broadcast([P, D, HC]), ALU.mult)
                last.then_inc(temp_step, 1)
                dve.wait_ge(temp_step, 3)

            for r in range(RING):
                last = nc.vector.memset(v_one[r][:], 1.0)
            last.then_inc(v_ones_set, 1)
            dve.wait_ge(weight_in["k"], 16)
            split_weight("k", wk)

            def low(kind, n, dst, src, hi_part):
                dve.wait_ge(hi[kind], n.count(1, 1))
                nc.vector.tensor_tensor(dst, src, hi_part, ALU.subtract).then_inc(emptied[kind], 1)

            def rest_of(kind, n, t, rest, w, bias):
                at_least(dve, lowest[kind], (n + -1).count(1, 1))
                dve.wait_ge(hi[kind], n.count(1, 1))
                for c in range(CC):
                    last = nc.vector.scalar_tensor_tensor(rest[:, c], bank_of(kind, 0)[:, c * w:(c + 1) * w], bias[:, c:c + 1],
                                                          t[:, 0, c], ALU.add, ALU.subtract)
                last.then_inc(emptied[kind], 1)

            def norm_stats(which, src, n, stats_sem):
                for t in range(QT):
                    last = nc.vector.bn_stats(stats[:, which, t], src[:, t])
                last.then_inc(stats_sem, 1)

            def norm_var(which, n, var_sem):
                for t in range(QT):
                    last = nc.vector.bn_aggr(meanvar[:, which, t], stats[:, which, t])
                last.then_inc(var_sem, 1)

            def flat(t):
                return t.rearrange("p c q -> p (c q)")

            def down(n, t):
                dve.wait_ge(full["down"], n.count(QT, t + 1))
                if t == 0:
                    at_least(dve, stored[n.slot], (n + -RING).slot_count(1, 2) * 16)
                nc.vector.scalar_tensor_tensor(y[:, n.slot, t], bank_of("down", t)[:, 0:C], 0.5 * DEQ * DEQ * DEQ, x1[:, n.slot, t],
                                               ALU.mult, ALU.add).then_inc(emptied["down"], 1)

            def look_for_wide(w, k):
                dve.wait_ge(gint_lo, k + 1)
                nc.vector.tensor_reduce(wide_max[:, k:k + 1], w[:, 1].bitcast(F32).rearrange("p c n -> p (c n)"), AX.X, ALU.max,
                                        apply_absolute_value=True).then_inc(wide_got, 1)

            def tell_if_wide():
                dve.wait_ge(wide_got, 3)
                nc.vector.reduce_max(wide_any[:], wide_max[:], AX.X).then_inc(wide_got, 1)
                dve.wait_ge(wide_got, 4)
                dve.wait_ge(consts_done, 1)
                nc.vector.tensor_scalar(wide_any[:], wide_any[:], 0.0, None, ALU.is_gt).then_inc(wide_col, 1)

            def turn(i):
                if i.loop is None and i.c == -2:
                    scale_query_weight()
                    split_weight("q", wq)
                if i.loop is None and i.c == -1:
                    dve.wait_ge(weight_in["o"], 16)
                    split_weight("o", wo)
                for g in range(STEPS):
                    if g == 6 and i.loop is None and i.c == 1:
                        tell_if_wide()
                    if i.loop is None and i.c == 1 and g == STEPS - 1:
                        dve.wait_ge(wide_sum, 1)
                        nc.vector.tensor_copy(wide_int[:], ps_a[0:1, 0:1]).then_inc(wide_set, 1)
                    n, ga = first_pass(i, g)
                    if n.exists(NB):
                        if ga == 0:
                            at_least(dve, full["shift"], (n + -RING).count(1, 1))
                        dve.wait_ge(a_full, n.count(STEPS, ga + 1))
                        qt, h0 = ga * AG // H, ga * AG % H
                        nc.vector.tensor_reduce(negmax[:, n.slot, qt, h0:h0 + AG], ps_a[:, 0:AG * NKV].rearrange("p (h k) -> p h k", h=AG),
                                                AX.X, ALU.max, negate=True).then_inc(a_max, 1)
                    if g == 0 and (i + 2).exists(NB):
                        rest_of("k", i + 2, k3, k_rest, NKV, bk_col)
                    if g == 1 and (i + -2).exists(NB):
                        m = i + -2
                        dve.wait_ge(full["wo"], m.count(1, 1))
                        dve.wait_ge(xres_done, m.count(1, 1))
                        if m.c == 0:
                            dve.wait_ge(gint_lo, 3)
                        nc.vector.tensor_tensor(flat(x1[:, m.slot]), bank_of("wo", 0)[:], flat(x_res[:, m.slot]), ALU.add).then_inc(emptied["wo"], 1)
                    if g == 2 and (i + -2).exists(NB):
                        m = i + -2
                        dve.wait_ge(emptied["wo"], m.count(1, 1))
                        norm_stats(1, x1[:, m.slot], m, stats2)
                        dve.wait_ge(stats2, m.count(1, 1))
                    if g == 3 and i.loop is None and -1 <= i.c <= 1:
                        look_for_wide((wg, wu, wd)[i.c + 1], i.c + 1)
                    if g == 1 and i.loop is None and i.c == FIRST + 1:
                        dve.wait_ge(weight_in["v"], 16)
                        split_weight("v", wv)
                    if g == 3 and (i + 3).exists(NB):
                        m = i + 3
                        dve.wait_ge(x_in[m.slot], m.slot_count(1, 1) * 16)
                        norm_stats(0, x_tok[:, m.slot], m, stats1)
                        dve.wait_ge(stats1, m.count(1, 1))
                    if g == 3 and (i + -3).exists(NB):
                        m, f = i + -3, FC - 1
                        dve.wait_ge(hi["hid"], m.count(FC, FC))
                        nc.vector.tensor_tensor(hidT[:, 1, f], hid[:, f % 2], hidT[:, 0, f].bitcast(F32), ALU.subtract).then_inc(hid_lo_last, 1)
                    if g == 3 and (i + 2).exists(NB):
                        rest_of("q", i + 2, q3, q_rest, NQ, bq_col)
                    if g == 4 and (i + 3).exists(NB):
                        norm_var(0, i + 3, var1)
                    if (g == 4 or g == 5) and (i + -3).exists(NB):
                        down(i + -3, g - 4)
                    if g == 4 and (i + -2).exists(NB):
                        low("normT2", i + -2, flat(xn2T[:, 1]), bank_of("normT2", 0)[:], flat(xn2T[:, 0]).bitcast(F32))
                    if g == 4 and (i + 2).exists(NB):
                        m = i + 2
                        if m.c == 0:
                            dve.wait_ge(v_ones_set, 1)
                            dve.wait_ge(bias_in, 16 * 2)
                        at_least(dve, pv_done, (m + -RING).count(PV, PV))
                        dve.wait_ge(full["v"], m.count(1, 1))
                        nc.vector.tensor_tensor(v_one[m.slot][:, :, 0:D], bank_of("v", 0)[0:NKV, 0:C].rearrange("p (h d) -> p h d", d=D),
                                                bv_row[0:NKV].rearrange("p (h d) -> p h d", d=D), ALU.add).then_inc(emptied["v"], 1)
                    if g == 6 and (i + -1).exists(NB):
                        m = i + -1
                        at_least(dve, full["attT"], (m + -1).count(1, 1))
                        for t in range(QT):
                            o = bank_of("attQ", t)[:].rearrange("p (h v) -> p h v", v=VW)
                            dve.wait_ge(full["attQ"], m.count(QT, t + 1))
                            nc.vector.reciprocal(rsum[:, t], o[:, :, D]).then_inc(rsum_done, 1)
                            dve.wait_ge(rsum_done, m.count(QT, t + 1))
                            nc.vector.tensor_tensor(att[:, t].rearrange("p (h d) -> p h d", d=D), o[:, :, 0:D],
                                                    rsum[:, t].unsqueeze(2).to_broadcast([P, H, D]), ALU.mult).then_inc(emptied["attQ"], 1)
                    if g == 2 and (i + -2).exists(NB) and not (i + -3).exists(NB):
                        norm_var(1, i + -2, var2)
                    n, f = hidden_chunk(i, g)
                    if n and n.exists(NB):
                        ps = bank_of("gateup", f)
                        wait_hidden_lo(dve, n, f - 2)
                        dve.wait_ge(tanh_done, n.count(FC, f + 1))
                        nc.vector.scalar_tensor_tensor(hid[:, f % 2], tanh_g[:, f % 2], 1.0, ps[:, 0:NQ], ALU.add, ALU.mult).then_inc(gated_done, 1)
                        if g == 2 and (i + -2).exists(NB):
                            norm_var(1, i + -2, var2)
                        dve.wait_ge(gated_done, n.count(FC, f + 1))
                        nc.vector.tensor_tensor(hid[:, f % 2], hid[:, f % 2], ps[:, NQ:2 * NQ], ALU.mult).then_inc(emptied["gateup"], 1)
                    if g == 1 and i.exists(NB):
                        low("shift", i, shiftT[:, 1], bank_of("shift", 0)[0:H, 0:NQ], shiftT[:, 0])
                    if g == 0 and (i + 2).exists(NB):
                        low("normT1", i + 2, flat(xn1T[:, 1]), bank_of("normT1", 0)[:], flat(xn1T[:, 0]).bitcast(F32))
                    if g == 7 and (i + -1).exists(NB):
                        low("attT", i + -1, flat(attT[:, 1]), bank_of("attT", 0)[:], flat(attT[:, 0]).bitcast(F32))

            turns(dve, turn)

        @block.tensor
        def _(pe):
            PARTS = [(0, 0), (1, 0), (0, 1)]

            pe.wait_ge(ident_done, 2)

            def product(dst, pairs):
                for k, (lhsT, rhs) in enumerate(pairs):
                    last = nc.tensor.matmul(dst, lhsT, rhs, start=(k == 0), stop=(k == len(pairs) - 1))
                return last

            def add(terms, start=False, stop=False):
                for k, (dst, lhsT, rhs) in enumerate(terms):
                    last = nc.tensor.matmul(dst, lhsT, rhs, start=(start and k == 0), stop=(stop and k == len(terms) - 1), skip_group_check=True)
                return last

            def add_if_wide(terms):
                with pe.If(wide[0] != 0):
                    add(terms)

            def transposes(ps, src):
                for c in range(CC):
                    for t in range(QT):
                        last = nc.tensor.transpose(ps[:, c * NQ + t * P:c * NQ + (t + 1) * P], src[:, t, c * P:(c + 1) * P], ident[:])
                return last

            def job(kind, idx, n, ps):
                if kind == "shift":
                    pe.wait_ge(a_max, n.count(STEPS, STEPS))
                    for t in range(QT):
                        last = nc.tensor.transpose(ps[0:H, t * P:(t + 1) * P], negmax[:, n.slot, t], ident[:])
                elif kind == "normT1":
                    pe.wait_ge(xn1_done, n.count(1, 1))
                    last = transposes(ps, xn1)
                elif kind == "normT2":
                    pe.wait_ge(xn2_done, n.count(1, 1))
                    last = transposes(ps, xn2)
                elif kind == "attT":
                    pe.wait_ge(emptied["attQ"], n.count(QT, QT))
                    last = transposes(ps, att)
                elif kind == "attQ":
                    if idx == 0:
                        pe.wait_ge(pv_copied, n.count(1, 1))
                    for k in range(PV):
                        last = nc.tensor.transpose(ps[:, k * P:(k + 1) * P], pv_T[:, k, idx * P:(idx + 1) * P], ident[:])
                elif kind == "q":
                    if n.c == 0:
                        pe.wait_ge(w_ready["q"], 2)
                    pe.wait_ge(emptied["normT1"], n.count(1, 1))
                    for m in range(CC):
                        last = product(ps[:, m * NQ:(m + 1) * NQ],
                                       [(wq[:, a, c, m * P:(m + 1) * P], xn1T[:, b, c]) for a, b in PARTS for c in range(CC)])
                elif kind == "k":
                    if n.c == 0:
                        pe.wait_ge(w_ready["k"], 2)
                    pe.wait_ge(ctx_lo, n.count(1, 1))
                    for m in range(CC):
                        last = product(ps[:, m * NKV:(m + 1) * NKV],
                                       [(wk[:, a, c, m * P:(m + 1) * P], ctxT[:, b, c]) for a, b in PARTS for c in range(CC)])
                elif kind == "v":
                    if n.c == 0:
                        pe.wait_ge(w_ready["v"], 2)
                    last = product(ps[0:NKV, 0:C], [(ctxT[:, a, c], wv[:, b, c]) for a, b in PARTS for c in range(CC)])
                elif kind == "wo":
                    if n.c == 0:
                        pe.wait_ge(w_ready["o"], 2)
                    pe.wait_ge(emptied["attT"], n.count(1, 1))
                    for t in range(QT):
                        last = product(ps[:, t * C:(t + 1) * C],
                                       [(attT[:, a, c, t * P:(t + 1) * P], wo[:, b, c]) for a, b in PARTS for c in range(CC)])
                elif kind == "gateup":
                    if idx == 0:
                        pe.wait_ge(emptied["normT2"], n.count(1, 1))

                    def terms(parts, c):
                        return [(ps[:, k * NQ:(k + 1) * NQ], w[:, a, c, idx * P:(idx + 1) * P], xn2T[:, b, c]) for a, b in parts for k, w in enumerate((wg, wu))]

                    add(terms([(0, 0)], 0), start=True)
                    add_if_wide(terms([(1, 0)], 0) + terms([(1, 0)], 1))
                    last = add(terms([(0, 0)], 1) + terms([(0, 1)], 0) + terms([(0, 1)], 1), stop=True)
                elif kind == "down":
                    def terms(parts, f):
                        return [(ps[:, 0:C], hidT[:, a, f, idx * P:(idx + 1) * P], wd[:, b, f]) for a, b in parts]

                    for f in range(FC):
                        if idx == 0:
                            wait_hidden_lo(pe, n, f)
                        if f == FC - 1:
                            add_if_wide([term for c in range(FC) for term in terms([(0, 1)], c)])
                        last = add(terms([(0, 0), (1, 0)], f), start=(f == 0), stop=(f == FC - 1))
                last.then_inc(full[kind], 1)

            wide = []

            def turn(i):
                for g in range(STEPS):
                    if i.loop is None and i.c == 1 and g == STEPS - 1:
                        pe.wait_ge(wide_col, 1)
                        pe.wait_ge(a_max, (i + 1).count(STEPS, g - 2))
                        nc.tensor.matmul(ps_a[0:1, 0:1], wide_any[:], ones_col[:], start=True, stop=True).then_inc(wide_sum, 1)
                        pe.wait_ge(wide_set, 1)
                        wide.append(pe.value_load(wide_int[0:1, 0:1]))
                    n, ga = first_pass(i, g)
                    if n.exists(NB):
                        if ga == 0:
                            pe.wait_ge(qs_in[n.slot], n.slot_count(1, 1) * (6 * 16))
                            pe.wait_ge(ks_in[n.slot], n.slot_count(1, 1) * (6 * 16))
                        at_least(pe, a_max, n.count(STEPS, ga))
                        qt, h0 = ga * AG // H, ga * AG % H
                        for k in range(AG):
                            last = nc.tensor.matmul(ps_a[:, k * NKV:(k + 1) * NKV], qs[n.slot][0:KS_ROWS, h0 + k, qt * P:(qt + 1) * P],
                                                    ks[n.slot][0:KS_ROWS, h0 + k], start=True, stop=True)
                        last.then_inc(a_full, 1)
                    n, gb = second_pass(i, g)
                    if n.exists(NB):
                        if gb == 0 and n.c == 0:
                            pe.wait_ge(k_ones_set, 1)
                        if gb == 0:
                            pe.wait_ge(shift_in[n.slot], n.slot_count(1, 1) * 32)
                        at_least(pe, exp_done, n.count(STEPS, gb))
                        for k in range(HG):
                            last = nc.tensor.matmul(ps_b[0:NKV, k * NQ:(k + 1) * NQ], ks[n.slot][:, gb * HG + k], qs[n.slot][:, gb * HG + k],
                                                    start=True, stop=True)
                        last.then_inc(b_full, 1)
                    for pos, (step, kind, idx, off, bank) in enumerate(JOBS):
                        if step == g and (i + off).exists(NB):
                            before = job_before(pos, i)
                            if before:
                                pe.wait_ge(emptied[before[0]], job_count(*before))
                            job(kind, idx, i + off, ps_w[bank])
                    n, gb = (n, gb - 1) if gb else (n + -1, STEPS - 1)
                    if gb % 2 and n.exists(NB):
                        pe.wait_ge(exp_done, n.count(STEPS, gb + 1))
                        if gb == 1:
                            pe.wait_ge(emptied["v"], n.count(1, 1))
                            at_least(pe, pv_copied, (n + -1).count(1, 1))
                        for k in range(HQ):
                            last = nc.tensor.matmul(ps_o[k * VW:(k + 1) * VW, gb // 2], v_one[n.slot][:, gb // 2 * HQ + k],
                                                    probs[0:NKV, (gb - 1 + k // HG) % 4, k % HG * NQ:(k % HG + 1) * NQ], start=True, stop=True)
                        last.then_inc(pv_done, 1)

            turns(pe, turn)


_ORDER = ["x", "ctx", "wqT", "bq", "wkT", "bk", "wvT", "bv", "woT", "bo", "temp", "tempc", "wgT", "wuT", "wdT"]


def kernel(**inputs):
    import numpy as np
    import concourse.bacc as bacc
    from concourse.bass_utils import run_bass_kernel_spmd as run

    a = {k.replace("L0_xattn_", "").replace("L0_ffn_", ""): np.asarray(v) for k, v in inputs.items()}
    heads = a["temperature"].size
    d = a["Wq"].shape[0] // heads

    def by_depth(v):
        return v.reshape(*v.shape[:-1], -1, P // d, d).swapaxes(-1, -2).reshape(v.shape)

    def chunks(v):
        return by_depth(v).reshape(-1, P).T

    def head_order(v):
        return v.reshape(-1, P // d, d, *v.shape[1:]).swapaxes(0, 1).reshape(v.shape)

    data = {
        "x": a["x"], "ctx": a["ctx_1024"].transpose(0, 2, 1),
        "wqT": by_depth(a["Wq"].T), "bq": chunks(a["bq"]), "wkT": by_depth(a["Wk"].T), "bk": chunks(a["bk"]), "wvT": head_order(a["Wv"]).T, "bv": head_order(a["bv"]),
        "woT": head_order(a["Wo"].T), "bo": a["bo"], "temp": a["temperature"],
        "tempc": chunks(np.repeat(a["temperature"], d)),
        "wgT": a["w_gate"].T, "wuT": a["w_up"].T, "wdT": a["w_down"].T,
    }
    data = {k: np.ascontiguousarray(v) for k, v in data.items()}
    nc = bacc.Bacc("TRN2", target_bir_lowering=False, num_devices=1)
    args = [nc.dram_tensor(k, data[k].shape, mybir.dt.from_np(data[k].dtype), kind="ExternalInput").ap() for k in _ORDER]
    y = nc.dram_tensor("out", data["x"].shape, F32, kind="ExternalOutput").ap()
    build(nc, *args, y)
    r = run(nc, [data], core_ids=[0])
    return r.results[0]["out"]
```
